# Optimizing a Trainium2 kernel written in Bass

```python
import numpy as np
import jax
import jax.numpy as jnp

def _softmax(x, axis=-1):
    return jax.nn.softmax(x, axis=axis)

def _gelu(x):
    return jax.nn.gelu(x, approximate=True)

def _silu(x):
    return jax.nn.silu(x)

def _sigmoid(x):
    return jax.nn.sigmoid(x)

def _layernorm(x, axis=-1, eps=1e-05):
    m = jnp.mean(x, axis=axis, keepdims=True)
    v = jnp.var(x, axis=axis, keepdims=True)
    return (x - m) / jnp.sqrt(v + eps)

def _scatter_add(tgt, idx, src, axis=0):
    return tgt.at[idx].add(src)

def _segment_sum(src, seg, n):
    return jax.ops.segment_sum(src, seg, n)
kernel_name = 'mk_xattn_seq_d2_seqx_r8_d783a1'

def setup_inputs(seed: int=0):
    np.random.seed(seed)
    _w = jnp.asarray

    def _rec_inputs():
        import jax
        import jax.numpy as jnp
        _rk = jax.random.key(seed)
        x = -0.0002928 + 1 * jax.random.normal(jax.random.fold_in(_rk, 1), (4, 512, 128), jnp.float32)
        _lenS = 512 - jax.random.randint(jax.random.fold_in(_rk, 7), (4,), 0, max(1, 512 // 4) + 1, jnp.int32)
        _lenS2 = 154 - jax.random.randint(jax.random.fold_in(_rk, 8), (4,), 0, max(1, 154 // 4) + 1, jnp.int32)
        _ctx_768P = jax.random.normal(jax.random.fold_in(_rk, 11), (4, 16, 96), jnp.float32)
        _ctx_768c = jax.random.dirichlet(jax.random.fold_in(_rk, 511), 0.3 * jnp.ones((16,), jnp.float32), (4, 154))
        _ctx_768t = jnp.einsum('bsk,bkd->bsd', _ctx_768c, _ctx_768P)
        _ctx_768t = _ctx_768t * jax.lax.rsqrt(jnp.mean(jnp.square(_ctx_768t)) + 1e-12) * 0.953939
        ctx_768 = 0.00095986 + 0.999812 * (_ctx_768t + 0.3 * jax.random.normal(jax.random.fold_in(_rk, 611), (4, 154, 96), jnp.float32))
        return (x, ctx_768)
    x, ctx_768 = _rec_inputs()

    def _L0_xattn_setup():
        import jax, jax.numpy as jnp
        import numpy as np
        B, S, L = (2, 256, 64)
        WIDTH, HEADS, CTX = (128, 16, 96)
        HD = WIDTH // HEADS
        EPS = 1e-05

        def _layernorm(x, g, b):
            m = jnp.mean(x, axis=-1, keepdims=True)
            v = jnp.mean(jnp.square(x - m), axis=-1, keepdims=True)
            return (x - m) * jax.lax.rsqrt(v + EPS) * g + b

        def _mha(q_in, kv_in, wq, bq, wk, bk, wv, bv, wo, bo):
            b = q_in.shape[0]
            q = (q_in @ wq.T + bq).reshape(b, -1, HEADS, HD).transpose(0, 2, 1, 3)
            k = (kv_in @ wk.T + bk).reshape(b, -1, HEADS, HD).transpose(0, 2, 1, 3)
            v = (kv_in @ wv.T + bv).reshape(b, -1, HEADS, HD).transpose(0, 2, 1, 3)
            scores = jnp.einsum('bhqd,bhkd->bhqk', q, k) * HD ** (-0.5)
            p = jax.nn.softmax(scores, axis=-1)
            o = jnp.einsum('bhqk,bhkd->bhqd', p, v)
            o = o.transpose(0, 2, 1, 3).reshape(b, -1, WIDTH)
            return o @ wo.T + bo
        key = jax.random.key(seed)
        ks = jax.random.split(key, 32)

        def xav(k, shape, gain=1.0):
            fan_out, fan_in = shape
            a = gain * np.sqrt(6.0 / (fan_in + fan_out))
            return jax.random.uniform(k, shape, jnp.float32, -a, a)
        g2 = 1.0 / np.sqrt(2.0)
        inp = {'x': jax.random.normal(ks[0], (B, S, WIDTH), jnp.float32), 'context': jax.random.normal(ks[1], (B, L, CTX), jnp.float32), 'ln1_g': jnp.ones((WIDTH,), jnp.float32), 'ln1_b': jnp.zeros((WIDTH,), jnp.float32), 'ln2_g': jnp.ones((WIDTH,), jnp.float32), 'ln2_b': jnp.zeros((WIDTH,), jnp.float32), 'ln3_g': jnp.ones((WIDTH,), jnp.float32), 'ln3_b': jnp.zeros((WIDTH,), jnp.float32), 'sa_wq': xav(ks[2], (WIDTH, WIDTH), g2), 'sa_bq': jnp.zeros((WIDTH,), jnp.float32), 'sa_wk': xav(ks[3], (WIDTH, WIDTH), g2), 'sa_bk': jnp.zeros((WIDTH,), jnp.float32), 'sa_wv': xav(ks[4], (WIDTH, WIDTH), g2), 'sa_bv': jnp.zeros((WIDTH,), jnp.float32), 'sa_wo': xav(ks[5], (WIDTH, WIDTH), 1.0), 'sa_bo': jnp.zeros((WIDTH,), jnp.float32), 'ca_wq': xav(ks[6], (WIDTH, WIDTH), g2), 'ca_bq': jnp.zeros((WIDTH,), jnp.float32), 'ca_wk': xav(ks[7], (WIDTH, CTX), g2), 'ca_bk': jnp.zeros((WIDTH,), jnp.float32), 'ca_wv': xav(ks[8], (WIDTH, CTX), g2), 'ca_bv': jnp.zeros((WIDTH,), jnp.float32), 'ca_wo': xav(ks[9], (WIDTH, WIDTH), 1.0), 'ca_bo': jnp.zeros((WIDTH,), jnp.float32), 'mlp_w1': 0.02 * jax.random.normal(ks[10], (4 * WIDTH, WIDTH), jnp.float32), 'mlp_b1': jnp.zeros((4 * WIDTH,), jnp.float32), 'mlp_w2': 0.02 * jax.random.normal(ks[11], (WIDTH, 4 * WIDTH), jnp.float32), 'mlp_b2': jnp.zeros((WIDTH,), jnp.float32)}
        return inp
    _L0_xattn_all = _L0_xattn_setup()
    _L0_xattn_in = {k: v for k, v in _L0_xattn_all.items() if k in ('ln1_g', 'ln1_b', 'ln2_g', 'ln2_b', 'ln3_g', 'ln3_b', 'sa_wq', 'sa_bq', 'sa_wk', 'sa_bk', 'sa_wv', 'sa_bv', 'sa_wo', 'sa_bo', 'ca_wq', 'ca_bq', 'ca_wk', 'ca_bk', 'ca_wv', 'ca_bv', 'ca_wo', 'ca_bo', 'mlp_w1', 'mlp_b1', 'mlp_w2', 'mlp_b2')}
    del _L0_xattn_all

    def _L1_xattn_setup():
        import jax, jax.numpy as jnp
        import numpy as np
        HEADS = 16
        D_HEAD = 64
        EPS = 1e-05

        def _ln(x, g, b):
            m = jnp.mean(x, axis=-1, keepdims=True)
            v = jnp.var(x, axis=-1, keepdims=True)
            return (x - m) * jax.lax.rsqrt(v + EPS) * g + b

        def _attn(xq, xc, Wq, Wk, Wv, Wo, bo):
            B, N, _ = xq.shape
            S = xc.shape[1]
            q = (xq @ Wq).reshape(B, N, HEADS, D_HEAD)
            k = (xc @ Wk).reshape(B, S, HEADS, D_HEAD)
            v = (xc @ Wv).reshape(B, S, HEADS, D_HEAD)
            scale = D_HEAD ** (-0.5)
            scores = jnp.einsum('bnhd,bshd->bhns', q, k) * scale
            attn = jax.nn.softmax(scores, axis=-1)
            out = jnp.einsum('bhns,bshd->bnhd', attn, v).reshape(B, N, HEADS * D_HEAD)
            return out @ Wo + bo

        def _geglu_ff(x, Wp, bp, Wf, bf):
            h = x @ Wp + bp
            a, gate = jnp.split(h, 2, axis=-1)
            return a * jax.nn.gelu(gate, approximate=False) @ Wf + bf
        key = jax.random.key(seed)
        ks = jax.random.split(key, 16)
        dim, ctx, inner, ffin = (128, 96, HEADS * D_HEAD, 4 * 128)

        def w(k, i, o):
            return jax.random.normal(k, (i, o), jnp.float32) * i ** (-0.5)
        inp = {'x': jax.random.normal(ks[0], (4, 256, dim), jnp.float32), 'context': jax.random.normal(ks[1], (4, 77, ctx), jnp.float32), 'Wq1': w(ks[2], dim, inner), 'Wk1': w(ks[3], dim, inner), 'Wv1': w(ks[4], dim, inner), 'Wo1': w(ks[5], inner, dim), 'bo1': jnp.zeros((dim,), jnp.float32), 'Wq2': w(ks[6], dim, inner), 'Wk2': w(ks[7], ctx, inner), 'Wv2': w(ks[8], ctx, inner), 'Wo2': w(ks[9], inner, dim), 'bo2': jnp.zeros((dim,), jnp.float32), 'Wp': w(ks[10], dim, 2 * ffin), 'bp': jnp.zeros((2 * ffin,), jnp.float32), 'Wf': w(ks[11], ffin, dim), 'bf': jnp.zeros((dim,), jnp.float32), 'g1': jnp.ones((dim,), jnp.float32), 'b1': jnp.zeros((dim,), jnp.float32), 'g2': jnp.ones((dim,), jnp.float32), 'b2': jnp.zeros((dim,), jnp.float32), 'g3': jnp.ones((dim,), jnp.float32), 'b3': jnp.zeros((dim,), jnp.float32)}
        return inp
    _L1_xattn_all = _L1_xattn_setup()
    _L1_xattn_in = {k: v for k, v in _L1_xattn_all.items() if k in ('Wq1', 'Wk1', 'Wv1', 'Wo1', 'bo1', 'Wq2', 'Wk2', 'Wv2', 'Wo2', 'bo2', 'Wp', 'bp', 'Wf', 'bf', 'g1', 'b1', 'g2', 'b2', 'g3', 'b3')}
    del _L1_xattn_all
    return {'x': x, 'ctx_768': ctx_768, 'L0_xattn_ln1_g': _L0_xattn_in['ln1_g'], 'L0_xattn_ln1_b': _L0_xattn_in['ln1_b'], 'L0_xattn_ln2_g': _L0_xattn_in['ln2_g'], 'L0_xattn_ln2_b': _L0_xattn_in['ln2_b'], 'L0_xattn_ln3_g': _L0_xattn_in['ln3_g'], 'L0_xattn_ln3_b': _L0_xattn_in['ln3_b'], 'L0_xattn_sa_wq': _L0_xattn_in['sa_wq'], 'L0_xattn_sa_bq': _L0_xattn_in['sa_bq'], 'L0_xattn_sa_wk': _L0_xattn_in['sa_wk'], 'L0_xattn_sa_bk': _L0_xattn_in['sa_bk'], 'L0_xattn_sa_wv': _L0_xattn_in['sa_wv'], 'L0_xattn_sa_bv': _L0_xattn_in['sa_bv'], 'L0_xattn_sa_wo': _L0_xattn_in['sa_wo'], 'L0_xattn_sa_bo': _L0_xattn_in['sa_bo'], 'L0_xattn_ca_wq': _L0_xattn_in['ca_wq'], 'L0_xattn_ca_bq': _L0_xattn_in['ca_bq'], 'L0_xattn_ca_wk': _L0_xattn_in['ca_wk'], 'L0_xattn_ca_bk': _L0_xattn_in['ca_bk'], 'L0_xattn_ca_wv': _L0_xattn_in['ca_wv'], 'L0_xattn_ca_bv': _L0_xattn_in['ca_bv'], 'L0_xattn_ca_wo': _L0_xattn_in['ca_wo'], 'L0_xattn_ca_bo': _L0_xattn_in['ca_bo'], 'L0_xattn_mlp_w1': _L0_xattn_in['mlp_w1'], 'L0_xattn_mlp_b1': _L0_xattn_in['mlp_b1'], 'L0_xattn_mlp_w2': _L0_xattn_in['mlp_w2'], 'L0_xattn_mlp_b2': _L0_xattn_in['mlp_b2'], 'L1_xattn_Wq1': _L1_xattn_in['Wq1'], 'L1_xattn_Wk1': _L1_xattn_in['Wk1'], 'L1_xattn_Wv1': _L1_xattn_in['Wv1'], 'L1_xattn_Wo1': _L1_xattn_in['Wo1'], 'L1_xattn_bo1': _L1_xattn_in['bo1'], 'L1_xattn_Wq2': _L1_xattn_in['Wq2'], 'L1_xattn_Wk2': _L1_xattn_in['Wk2'], 'L1_xattn_Wv2': _L1_xattn_in['Wv2'], 'L1_xattn_Wo2': _L1_xattn_in['Wo2'], 'L1_xattn_bo2': _L1_xattn_in['bo2'], 'L1_xattn_Wp': _L1_xattn_in['Wp'], 'L1_xattn_bp': _L1_xattn_in['bp'], 'L1_xattn_Wf': _L1_xattn_in['Wf'], 'L1_xattn_bf': _L1_xattn_in['bf'], 'L1_xattn_g1': _L1_xattn_in['g1'], 'L1_xattn_b1': _L1_xattn_in['b1'], 'L1_xattn_g2': _L1_xattn_in['g2'], 'L1_xattn_b2': _L1_xattn_in['b2'], 'L1_xattn_g3': _L1_xattn_in['g3'], 'L1_xattn_b3': _L1_xattn_in['b3']}

def reference(x, ctx_768, L0_xattn_ln1_g, L0_xattn_ln1_b, L0_xattn_ln2_g, L0_xattn_ln2_b, L0_xattn_ln3_g, L0_xattn_ln3_b, L0_xattn_sa_wq, L0_xattn_sa_bq, L0_xattn_sa_wk, L0_xattn_sa_bk, L0_xattn_sa_wv, L0_xattn_sa_bv, L0_xattn_sa_wo, L0_xattn_sa_bo, L0_xattn_ca_wq, L0_xattn_ca_bq, L0_xattn_ca_wk, L0_xattn_ca_bk, L0_xattn_ca_wv, L0_xattn_ca_bv, L0_xattn_ca_wo, L0_xattn_ca_bo, L0_xattn_mlp_w1, L0_xattn_mlp_b1, L0_xattn_mlp_w2, L0_xattn_mlp_b2, L1_xattn_Wq1, L1_xattn_Wk1, L1_xattn_Wv1, L1_xattn_Wo1, L1_xattn_bo1, L1_xattn_Wq2, L1_xattn_Wk2, L1_xattn_Wv2, L1_xattn_Wo2, L1_xattn_bo2, L1_xattn_Wp, L1_xattn_bp, L1_xattn_Wf, L1_xattn_bf, L1_xattn_g1, L1_xattn_b1, L1_xattn_g2, L1_xattn_b2, L1_xattn_g3, L1_xattn_b3):
    import jax
    import jax.numpy as jnp

    def _L0_xattn_ref(x, context, ln1_g, ln1_b, ln2_g, ln2_b, ln3_g, ln3_b, sa_wq, sa_bq, sa_wk, sa_bk, sa_wv, sa_bv, sa_wo, sa_bo, ca_wq, ca_bq, ca_wk, ca_bk, ca_wv, ca_bv, ca_wo, ca_bo, mlp_w1, mlp_b1, mlp_w2, mlp_b2):
        import jax, jax.numpy as jnp
        import numpy as np
        B, S, L = (2, 256, 64)
        WIDTH, HEADS, CTX = (128, 16, 96)
        HD = WIDTH // HEADS
        EPS = 1e-05

        def _layernorm(x, g, b):
            m = jnp.mean(x, axis=-1, keepdims=True)
            v = jnp.mean(jnp.square(x - m), axis=-1, keepdims=True)
            return (x - m) * jax.lax.rsqrt(v + EPS) * g + b

        def _mha(q_in, kv_in, wq, bq, wk, bk, wv, bv, wo, bo):
            b = q_in.shape[0]
            q = (q_in @ wq.T + bq).reshape(b, -1, HEADS, HD).transpose(0, 2, 1, 3)
            k = (kv_in @ wk.T + bk).reshape(b, -1, HEADS, HD).transpose(0, 2, 1, 3)
            v = (kv_in @ wv.T + bv).reshape(b, -1, HEADS, HD).transpose(0, 2, 1, 3)
            scores = jnp.einsum('bhqd,bhkd->bhqk', q, k) * HD ** (-0.5)
            p = jax.nn.softmax(scores, axis=-1)
            o = jnp.einsum('bhqk,bhkd->bhqd', p, v)
            o = o.transpose(0, 2, 1, 3).reshape(b, -1, WIDTH)
            return o @ wo.T + bo
        h = _layernorm(x, ln1_g, ln1_b)
        x = x + _mha(h, h, sa_wq, sa_bq, sa_wk, sa_bk, sa_wv, sa_bv, sa_wo, sa_bo)
        h = _layernorm(x, ln2_g, ln2_b)
        x = x + _mha(h, context, ca_wq, ca_bq, ca_wk, ca_bk, ca_wv, ca_bv, ca_wo, ca_bo)
        h = _layernorm(x, ln3_g, ln3_b)
        h = jax.nn.gelu(h @ mlp_w1.T + mlp_b1, approximate=False) @ mlp_w2.T + mlp_b2
        return x + h

    def _L1_xattn_ref(x, context, Wq1, Wk1, Wv1, Wo1, bo1, Wq2, Wk2, Wv2, Wo2, bo2, Wp, bp, Wf, bf, g1, b1, g2, b2, g3, b3):
        import jax, jax.numpy as jnp
        import numpy as np
        HEADS = 16
        D_HEAD = 64
        EPS = 1e-05

        def _ln(x, g, b):
            m = jnp.mean(x, axis=-1, keepdims=True)
            v = jnp.var(x, axis=-1, keepdims=True)
            return (x - m) * jax.lax.rsqrt(v + EPS) * g + b

        def _attn(xq, xc, Wq, Wk, Wv, Wo, bo):
            B, N, _ = xq.shape
            S = xc.shape[1]
            q = (xq @ Wq).reshape(B, N, HEADS, D_HEAD)
            k = (xc @ Wk).reshape(B, S, HEADS, D_HEAD)
            v = (xc @ Wv).reshape(B, S, HEADS, D_HEAD)
            scale = D_HEAD ** (-0.5)
            scores = jnp.einsum('bnhd,bshd->bhns', q, k) * scale
            attn = jax.nn.softmax(scores, axis=-1)
            out = jnp.einsum('bhns,bshd->bnhd', attn, v).reshape(B, N, HEADS * D_HEAD)
            return out @ Wo + bo

        def _geglu_ff(x, Wp, bp, Wf, bf):
            h = x @ Wp + bp
            a, gate = jnp.split(h, 2, axis=-1)
            return a * jax.nn.gelu(gate, approximate=False) @ Wf + bf
        x = _attn(_ln(x, g1, b1), _ln(x, g1, b1), Wq1, Wk1, Wv1, Wo1, bo1) + x
        x = _attn(_ln(x, g2, b2), context, Wq2, Wk2, Wv2, Wo2, bo2) + x
        x = _geglu_ff(_ln(x, g3, b3), Wp, bp, Wf, bf) + x
        return x
    x = _L0_xattn_ref(x, ctx_768, L0_xattn_ln1_g, L0_xattn_ln1_b, L0_xattn_ln2_g, L0_xattn_ln2_b, L0_xattn_ln3_g, L0_xattn_ln3_b, L0_xattn_sa_wq, L0_xattn_sa_bq, L0_xattn_sa_wk, L0_xattn_sa_bk, L0_xattn_sa_wv, L0_xattn_sa_bv, L0_xattn_sa_wo, L0_xattn_sa_bo, L0_xattn_ca_wq, L0_xattn_ca_bq, L0_xattn_ca_wk, L0_xattn_ca_bk, L0_xattn_ca_wv, L0_xattn_ca_bv, L0_xattn_ca_wo, L0_xattn_ca_bo, L0_xattn_mlp_w1, L0_xattn_mlp_b1, L0_xattn_mlp_w2, L0_xattn_mlp_b2)
    x = _L1_xattn_ref(x, ctx_768, L1_xattn_Wq1, L1_xattn_Wk1, L1_xattn_Wv1, L1_xattn_Wo1, L1_xattn_bo1, L1_xattn_Wq2, L1_xattn_Wk2, L1_xattn_Wv2, L1_xattn_Wo2, L1_xattn_bo2, L1_xattn_Wp, L1_xattn_bp, L1_xattn_Wf, L1_xattn_bf, L1_xattn_g1, L1_xattn_b1, L1_xattn_g2, L1_xattn_b2, L1_xattn_g3, L1_xattn_b3)
    return x

_drawn_inputs = setup_inputs


def setup_inputs(seed=0):
    import zlib

    import numpy as np

    out = dict(_drawn_inputs(seed))
    spreads = {'L0_xattn_ln1_g': (1.0, 0.6),
     'L0_xattn_ln1_b': (0.0, 0.1),
     'L0_xattn_ln2_g': (1.0, 0.6),
     'L0_xattn_ln2_b': (0.0, 0.8),
     'L0_xattn_ln3_g': (1.0, 0.6),
     'L0_xattn_ln3_b': (0.0, 0.8),
     'L0_xattn_sa_bq': (0.0, 0.8),
     'L0_xattn_sa_bk': (0.0, 2.0),
     'L0_xattn_sa_bv': (0.0, 0.1),
     'L0_xattn_sa_bo': (0.0, 0.1),
     'L0_xattn_ca_bq': (0.0, 0.766),
     'L0_xattn_ca_bk': (0.0, 2.0),
     'L0_xattn_ca_bv': (0.0, 0.1),
     'L0_xattn_ca_bo': (0.0, 0.1),
     'L0_xattn_mlp_b1': (0.0, 0.28),
     'L0_xattn_mlp_b2': (0.0, 0.1),
     'L1_xattn_bo1': (0.0, 0.1),
     'L1_xattn_bo2': (0.0, 0.1),
     'L1_xattn_bp': (0.0, 0.1),
     'L1_xattn_bf': (0.0, 0.1),
     'L1_xattn_g1': (1.0, 0.2),
     'L1_xattn_b1': (0.0, 0.1),
     'L1_xattn_g2': (1.0, 0.2),
     'L1_xattn_b2': (0.0, 0.381),
     'L1_xattn_g3': (1.0, 0.2),
     'L1_xattn_b3': (0.0, 0.1)}
    factors = {}
    for name, (base, spread) in spreads.items():
        noise = np.random.default_rng([zlib.crc32(name.encode()), seed]).standard_normal(out[name].shape)
        drawn = base * np.exp(spread * noise) if base else spread * noise
        out[name] = jnp.asarray(drawn.astype(out[name].dtype))
    for name, factor in factors.items():
        out[name] = (out[name] * factor).astype(out[name].dtype)
    return out
```

```python
from contextlib import ExitStack

import concourse.bass as bass
from concourse import mybir

F32 = mybir.dt.float32
F32R = mybir.dt.float32r
ALU = mybir.AluOpType
ACT = mybir.ActivationFunctionType
AX = mybir.AxisListType

B, S, D = 4, 512, 128
SK, C = 154, 96
H = 16
HD = (8, 64)
INNER = H * HD[1]
F = 512
QT = S // 128
EPS = 1e-5
KT = {True: [(0, 128), (128, 128), (256, 128), (384, 128)], False: [(0, 128), (128, SK - 128)]}
ATT = [(0, True), (0, False), (1, True), (1, False)]
PHASES = [("att", 0), ("att", 1), ("mlp", 0), ("att", 2), ("att", 3), ("mlp", 1)]
UNITS = H * QT

FIELDS = [
    ("ln", 12),
    ("wq0", 512), ("bq0", 4), ("wk0", 512), ("bk0", 4), ("wv0", 128), ("bv0", 128), ("wo0", 512), ("bo0", 128),
    ("wq1", 512), ("bq1", 4), ("wk1", 512), ("bk1", 4), ("wv1", 128), ("bv1", 128), ("wo1", 512), ("bo1", 128),
    ("w1_0", 512), ("b1_0", 4), ("w2_0", 512), ("b2_0", 128),
    ("wq2", INNER), ("wk2", INNER), ("wv2", INNER), ("wo2", INNER), ("bo2", 128),
    ("wq3", INNER), ("wk3", INNER), ("wv3", INNER), ("wo3", INNER), ("bo3", 128),
    ("w1_1", 2 * F), ("b1_1", 8), ("w2_1", 512), ("b2_1", 128),
]
AT, _at = {}, 0
for _name, _w in FIELDS:
    AT[_name] = (_at, _at + _w)
    _at += _w
WCOLS = _at
PARTS = [("ln", "wq1"), ("wq1", "w1_0"), ("w1_0", "wq2"), ("wq2", "wq3"), ("wq3", "w1_1"), ("w1_1", None)]
PART_OF_PHASE = {("att", 0): 0, ("att", 1): 1, ("mlp", 0): 2, ("att", 2): 3, ("att", 3): 4, ("mlp", 1): 5}


def steps(a):
    return 4 if ATT[a][0] == 0 else H


def v_jobs(a):
    layer, own = ATT[a]
    if layer == 0:
        return [("v", a, 0)]
    return [("v", a, 2 * n + half) for n in range(len(KT[own])) for half in range(2)]


def plan():
    jobs = []
    for n, (kind, a) in enumerate(PHASES):
        jobs.append((("ln", n), "dve"))
        if kind == "att":
            jobs += [(("q", a, 0), "dve"), (("k", a, 0), "dve")]
            jobs += [(j, "dve") for j in v_jobs(a)]
            for s in range(1, steps(a)):
                jobs += [(("q", a, s), "dve"), (("k", a, s), "dve")]
            jobs.append((("wo", a), "dve"))
        else:
            for m in range(4):
                jobs.append((("gelu", a, m), "act"))
                if a == 1:
                    jobs.append((("lin", a, m), "dve"))
            jobs.append((("y", a), "dve"))
    index, count, per = {}, {}, {"dve": 0, "act": 0}
    for n, (job, eng) in enumerate(jobs):
        per[eng] += 1
        index[job], count[job] = n, per[eng]
    return jobs, index, count, per


JOBS, INDEX, TAKEN, PER = plan()


def build(nc, x, ctx_t, wimg, out):
    with ExitStack() as ctx:
        def sb(name, shape, dt=F32):
            return ctx.enter_context(nc.sbuf_tensor(name, shape, dt))

        def psum(name, shape):
            return ctx.enter_context(nc.psum_tensor(name, shape, F32))

        def sem(name):
            return ctx.enter_context(nc.semaphore(name))

        w = sb("w", [128, WCOLS])
        ident = sb("ident", [128, 128])
        x_in = sb("x_in", [128, QT, D])
        xs = sb("xs", [128, QT, D])
        y_out = sb("y_out", [128, QT, D])
        c_t = sb("c_t", [C, SK])
        xn = sb("xn", [128, QT, D])
        stats = sb("stats", [128, QT, 6])
        mv = sb("mv", [128, QT, 2])
        var_eps = sb("var_eps", [128, QT])
        minus_half = sb("minus_half", [128, QT])
        rstd = sb("rstd", [128, QT])
        wait_taker = sb("wait_taker", [128, 1])
        h_t = sb("h_t", [128, S])
        q0 = sb("q0", [128, 2, S], F32R)
        k_parts = sb("k_parts", [128, 2, S], F32R)
        k0 = sb("k0", [128, 2, 4, S], F32R)
        v0 = sb("v0", [128, 4, H, 32])
        q_hi = sb("q_hi", [128, 2, S], F32R)
        q_lo = sb("q_lo", [128, 2, S], F32R)
        k1 = sb("k1", [128, 2, S], F32R)
        v1 = sb("v1", [128, 4, INNER])
        NP, NPT = 4, 3
        p = sb("p", [128, NP, S])
        p_t = sb("p_t", [128, NPT, 4, S])
        p_tx = sb("p_tx", [128, NPT, S])
        neg_max = sb("neg_max", [128, 4])
        row_sum = sb("row_sum", [128, 4])
        r_sum = sb("r_sum", [128, 4])
        o_t = sb("o_t", [128, 8, S])
        gate = sb("gate", [128, 2, S])

        NS, NT = 3, 2
        ps_s = psum("ps_s", [128, NS, 512])
        ps_t = psum("ps_t", [128, NT, 512])
        ps_o = psum("ps_o", [128, 512])
        ps_g = psum("ps_g", [128, 2, 512])

        w_loaded = [sem(f"w_loaded{n}") for n in range(len(PARTS))]
        x_loaded = sem("x_loaded")
        c_loaded = sem("c_loaded")
        ident_done = sem("ident_done")
        zeros_done = sem("zeros_done")
        scale_done = sem("scale_done")
        out_stored = sem("out_stored")
        stats_done = sem("stats_done")
        mv_done = sem("mv_done")
        var_done = sem("var_done")
        rstd_done = sem("rstd_done")
        norm_done = sem("norm_done")
        bias_added = sem("bias_added")
        gen_filled = sem("gen_filled")
        taken = {"dve": sem("taken_by_dve"), "act": sem("taken_by_act")}
        hi_done = sem("hi_done")
        k_spread = [sem("k_spread0"), sem("k_spread1")]
        scores_ready = sem("scores_ready")
        max_ready = sem("max_ready")
        exp_ready = sem("exp_ready")
        recip_done = sem("recip_done")
        probs_ready = sem("probs_ready")
        pt_filled = sem("pt_filled")
        pt_copied = sem("pt_copied")
        o_filled = sem("o_filled")
        o_copied = sem("o_copied")

        def W(name, lo=0, hi=None, rows=128):
            a, z = AT[name]
            return w[0:rows, a + lo:(z if hi is None else a + hi)]

        PER_SPLIT = sum(2 * steps(a) for a in range(4))
        PER_O = sum(4 if ATT[a][0] == 0 else 8 for a in range(4))
        PER_UNIT = 4 * UNITS
        N_LN = len(PHASES)

        def o_base(a):
            return sum(4 if ATT[n][0] == 0 else 8 for n in range(a))

        def wait_taken(eng, b, job):
            who = dict(JOBS)[job]
            eng.wait_ge(taken[who], b * PER[who] + TAKEN[job])

        def wait_filled(eng, b, job):
            eng.wait_ge(gen_filled, b * len(JOBS) + INDEX[job] + 1)

        def unit_wait(eng, semaphore, b, a, i):
            eng.wait_ge(semaphore, b * PER_UNIT + a * UNITS + i + 1)

        LAG_N, LAG_T, LAG_V = 1, 3, 4
        SLOTS = UNITS + LAG_V

        def job_slot(a, s):
            return UNITS // steps(a) * (s - 1) + 1

        def slot_jobs(a, i):
            for s in range(1, steps(a)):
                if job_slot(a, s) == i:
                    yield ("q", a, s)
                if job_slot(a, s) + 1 == i:
                    yield ("k", a, s)

        def heads_at(a, i):
            n = i - LAG_V + 1
            if ATT[a][0] == 0:
                return [n // QT - 1] if n > 0 and n % QT == 0 else []
            return [n // QT - 2, n // QT - 1] if n > 0 and n % (2 * QT) == 0 else []

        def out_set(a, h):
            per = 4 if ATT[a][0] == 0 else 2
            return h // per, h % per == per - 1

        block = ctx.enter_context(nc.Block())

        @block.sync
        def _(sp):
            for n, (first, end) in enumerate(PARTS):
                lo, hi = AT[first][0], (AT[end][0] if end else WCOLS)
                sp.dma_start(w[:, lo:hi], wimg[:, lo:hi]).then_inc(w_loaded[n], 16)
            with sp.Fori(0, B) as b:
                for a in range(2):
                    for g in range(4):
                        wait_taken(sp, b, ("k", a, g))
                        for j in range(4):
                            nk = S if ATT[a][1] else SK
                            sp.dma_start(k0[j:128:4, g % 2, j, 0:nk].bitcast(F32),
                                         k_parts[j:128:4, g % 2, 0:nk].bitcast(F32)).then_inc(k_spread[g % 2], 16)

        @block.gpsimd
        def _(pool):
            pool.dma_start(x_in[:], x[0].rearrange("(t p) d -> p t d", p=128)).then_inc(x_loaded, 16)
            pool.dma_start(c_t[:], ctx_t[0]).then_inc(c_loaded, 16)
            pool.memset(minus_half[:], -0.5).then_inc(ident_done, 1)
            pool.memset(ident[:], 0.0).then_inc(ident_done, 1)
            pool.wait_ge(ident_done, 2)
            pool.affine_select(out=ident[:], in_=ident[:], compare_op=ALU.not_equal, fill=1.0, base=0,
                               pattern=[[-1, 128]], channel_multiplier=1).then_inc(ident_done, 1)
            with pool.Fori(0, B) as b:
                for n, (kind, a) in enumerate(PHASES):
                    pool.wait_ge(var_done, b * N_LN + n + 1)
                    pool.tensor_tensor(rstd[:], var_eps[:], minus_half[:], ALU.pow).then_inc(rstd_done, 1)
                    pool.wait_ge(norm_done, b * N_LN + n + 1)
                    if n == 0:
                        pool.wait_ge(w_loaded[5], 16)
                        for part in range(5):
                            pool.wait_ge(w_loaded[part], 16)
                    bias = W(f"bo{a}") if kind == "att" else W(f"b2_{a}")
                    pool.tensor_tensor(xs[:], x_in[:] if n == 0 else xs[:],
                                       bias[:, None, :].to_broadcast([128, QT, D]), ALU.add).then_inc(bias_added, 1)
                    if n == 0:
                        pool.wait_ge(bias_added, b * N_LN + 1)
                        pool.dma_start(x_in[:], x[1:B + 1][b].rearrange("(t p) d -> p t d", p=128)).then_inc(x_loaded, 16)

                    if n == 4:
                        wait_taken(pool, b, ("k", 3, H - 1))
                        pool.dma_start(c_t[:], ctx_t[1:B + 1][b]).then_inc(c_loaded, 16)
                wait_taken(pool, b, ("y", 1))
                pool.dma_start(out[b].rearrange("(t p) d -> p t d", p=128), y_out[:]).then_inc(out_stored, 16)
                pool.wait_ge(out_stored, b * 16 + 16)
            pool.wait_ge(out_stored, 16 * B)
            pool.wait_ge(x_loaded, 16 * (B + 1))
            pool.wait_ge(c_loaded, 16 * (B + 1))

        @block.tensor
        def _(pe):
            def product(b, job, emit):
                n = INDEX[job]
                if n >= 2:
                    wait_taken(pe, b, JOBS[n - 2][0])
                emit(ps_g[:, n % 2, :]).then_inc(gen_filled, 1)

            def transposes(n):
                def emit(bank):
                    for t in range(QT):
                        last = pe.transpose(bank[:, 128 * t:128 * t + 128], xn[:, t, :], ident[:])
                    return last
                return emit

            def qk_product(kind, a, s):
                layer, own = ATT[a]
                if kind == "q" or own:
                    rows, src, nk = 128, h_t[:], S
                else:
                    rows, src, nk = C, c_t[:], SK

                def emit(bank):
                    if layer == 0:
                        return pe.matmul(bank[:, 0:nk], W(f"w{kind}{a}", 128 * s, 128 * s + 128, rows), src,
                                         start=True, stop=True)
                    for r in (0, 64):
                        last = pe.matmul(bank[r:r + 64, 0:nk], W(f"w{kind}{a}", 64 * s, 64 * s + 64, rows), src,
                                         start=True, stop=True)
                    return last
                return emit

            def v_product(a, n):
                layer, own = ATT[a]
                rows, src = (128, h_t) if own else (C, c_t)

                def emit(bank):
                    if layer == 0:
                        for kt, (k0_, kn) in enumerate(KT[own]):
                            last = pe.matmul(bank[0:kn, 128 * kt:128 * kt + 128], src[:, k0_:k0_ + kn],
                                             W(f"wv{a}", rows=rows), start=True, stop=True)
                        return last
                    k0_, kn = KT[own][n // 2]
                    half = n % 2
                    return pe.matmul(bank[0:kn, :], src[:, k0_:k0_ + kn],
                                     W(f"wv{a}", 512 * half, 512 * half + 512, rows), start=True, stop=True)
                return emit

            def step_product(b, job):
                kind, a, s = job
                product(b, job, qk_product(kind, a, s))

            def attention(b, n, a):
                layer, own = ATT[a]
                nk = S if own else SK
                if not own and layer == 0:
                    pe.wait_ge(c_loaded, b * 16 + 16)
                wait_taken(pe, b, ("ln", n))
                step_product(b, ("q", a, 0))
                step_product(b, ("k", a, 0))
                for job in v_jobs(a):
                    product(b, job, v_product(a, job[2]))
                for i in range(SLOTS):
                    if i < UNITS:
                        h, t = divmod(i, QT)
                        if t == 0:
                            s = h // (H // steps(a))
                            if h % (H // steps(a)) == 0:
                                wait_taken(pe, b, ("k", a, s))
                                if layer == 0:
                                    pe.wait_ge(k_spread[s % 2], b * 256 + 128 * a + 64 * (s // 2 + 1))
                        if i >= NS:
                            unit_wait(pe, exp_ready, b, a, i - NS)
                        bank = ps_s[:, i % NS, 0:nk]
                        if layer == 0:
                            s = h // 4
                            pe.matmul(bank, q0[:, s % 2, 128 * t:128 * t + 128], k0[:, s % 2, h % 4, 0:nk],
                                      start=True, stop=True).then_inc(scores_ready, 1)
                        else:
                            pe.matmul(bank, q_hi[:, h % 2, 128 * t:128 * t + 128], k1[:, h % 2, 0:nk],
                                      start=True, stop=False)
                            pe.matmul(bank, q_lo[:, h % 2, 128 * t:128 * t + 128], k1[:, h % 2, 0:nk],
                                      start=False, stop=True).then_inc(scores_ready, 1)
                    for job in slot_jobs(a, i):
                        step_product(b, job)
                    u = i - LAG_T
                    if 0 <= u < UNITS:
                        unit_wait(pe, probs_ready, b, a, u)
                        if u >= NT:
                            unit_wait(pe, pt_copied, b, a, u - NT)
                        for kt, (k0_, kn) in enumerate(KT[own]):
                            last = pe.transpose(ps_t[0:kn, u % NT, 128 * kt:128 * kt + 128],
                                                p[:, u % NP, k0_:k0_ + kn], ident[:])
                        last.then_inc(pt_filled, 1)
                    heads = heads_at(a, i)
                    if heads:
                        unit_wait(pe, pt_copied, b, a, QT * heads[-1] + QT - 1)
                        o_set, full = out_set(a, heads[-1])
                        first = out_set(a, heads[0] - 1)[1] if heads[0] else True
                        if i == LAG_V + QT * len(heads) - 1:
                            wait_taken(pe, b, v_jobs(a)[-1])
                        if first and o_set > 0:
                            pe.wait_ge(o_copied, b * PER_O + o_base(a) + o_set)
                        for kt in range(len(KT[own])):
                            for h in heads:
                                rhs = p_tx[:, h % NPT, :] if not own and kt == 1 else p_t[:, h % NPT, kt, :]
                                if layer == 0:
                                    last = pe.matmul(ps_o[32 * kt:32 * kt + 32, :], v0[:, kt, h, :], rhs,
                                                     start=h % 4 == 0, stop=h % 4 == 3, skip_group_check=True)
                                else:
                                    r = 64 * (h % 2)
                                    last = pe.matmul(ps_o[r:r + 64, :], v1[:, kt, 64 * h:64 * h + 64], rhs,
                                                     start=kt == 0, stop=kt == len(KT[own]) - 1)
                        if full:
                            last.then_inc(o_filled, 1)

                def output(bank):
                    sets = 4 if layer == 0 else 8
                    rows = 128 if layer == 1 else 32 * len(KT[own])
                    for t in range(QT):
                        for s in range(sets):
                            last = pe.matmul(bank[:, 128 * t:128 * t + 128], o_t[0:rows, s, 128 * t:128 * t + 128],
                                             W(f"wo{a}", 128 * s, 128 * s + 128, rows),
                                             start=s == 0, stop=s == sets - 1)
                    return last

                pe.wait_ge(o_copied, b * PER_O + o_base(a) + (4 if layer == 0 else 8))
                product(b, ("wo", a), output)

            def mlp(b, n, a):
                wait_taken(pe, b, ("ln", n))
                for m in range(4):
                    off = F if a == 1 else 0
                    product(b, ("gelu", a, m), lambda bank: pe.matmul(
                        bank, W(f"w1_{a}", off + 128 * m, off + 128 * m + 128), h_t[:], start=True, stop=True))
                    if a == 1:
                        product(b, ("lin", a, m), lambda bank: pe.matmul(
                            bank, W(f"w1_{a}", 128 * m, 128 * m + 128), h_t[:], start=True, stop=True))

                def output(bank):
                    for t in range(QT):
                        for m in range(4):
                            last = pe.matmul(bank[:, 128 * t:128 * t + 128], o_t[:, m, 128 * t:128 * t + 128],
                                             W(f"w2_{a}", 128 * m, 128 * m + 128), start=m == 0, stop=m == 3)
                    return last

                wait_taken(pe, b, ("gelu", 0, 3) if a == 0 else ("lin", 1, 3))
                product(b, ("y", a), output)

            pe.wait_ge(ident_done, 3)
            for part in range(len(PARTS)):
                pe.wait_ge(w_loaded[part], 16)
            pe.wait_ge(scale_done, 4)
            pe.wait_ge(zeros_done, 3)
            with pe.Fori(0, B) as b:
                for n, (kind, a) in enumerate(PHASES):
                    pe.wait_ge(norm_done, b * N_LN + n + 1)
                    product(b, ("ln", n), transposes(n))
                    (attention if kind == "att" else mlp)(b, n, a)

        @block.scalar
        def _(act):
            def attention(b, a):
                layer, own = ATT[a]
                nk = S if own else SK
                for i in range(SLOTS):
                    if i < UNITS:
                        unit_wait(act, max_ready, b, a, i)
                        if i >= NP:
                            unit_wait(act, pt_filled, b, a, i - NP)
                        act.activation(p[:, i % NP, 0:nk], ps_s[:, i % NS, 0:nk], ACT.Exp,
                                       bias=neg_max[:, i % 4:i % 4 + 1], scale=1.0,
                                       accum_out=row_sum[:, i % 4:i % 4 + 1]).then_inc(exp_ready, 1)
                    u = i - LAG_T
                    if 0 <= u < UNITS:
                        h, t = divmod(u, QT)
                        unit_wait(act, pt_filled, b, a, u)
                        if t == 0 and h >= NPT:
                            unit_wait(act, scores_ready, b, a, u)
                        cols = slice(128 * t, 128 * t + 128)
                        if own:
                            act.activation(p_t[:, h % NPT, :, cols],
                                           ps_t[:, u % NT, :].rearrange("k (n q) -> k n q", n=4),
                                           ACT.Copy).then_inc(pt_copied, 1)
                        else:
                            kn = SK - 128
                            act.activation(p_t[:, h % NPT, 0, cols], ps_t[:, u % NT, 0:128], ACT.Copy)
                            act.activation(p_tx[0:kn, h % NPT, cols], ps_t[0:kn, u % NT, 128:256],
                                           ACT.Copy).then_inc(pt_copied, 1)

            def mlp(b, a):
                for m in range(4):
                    wait_filled(act, b, ("gelu", a, m))
                    if a == 0:
                        dst = o_t[:, m, :]
                    else:
                        dst = gate[:, m % 2, :]
                        if m >= 2:
                            wait_taken(act, b, ("lin", 1, m - 2))
                    bias = W(f"b1_{a}", 4 * a + m, 4 * a + m + 1)
                    act.activation(dst, ps_g[:, INDEX[("gelu", a, m)] % 2, :], ACT.Gelu,
                                   bias=bias, scale=1.0).then_inc(taken["act"], 1)

            for part in (2, 5):
                act.wait_ge(w_loaded[part], 16)
            act.wait_ge(zeros_done, 3)
            with act.Fori(0, B) as b:
                for kind, a in PHASES:
                    (attention if kind == "att" else mlp)(b, a)

        @block.vector
        def _(dve):
            splits = [0]

            def split_wait(b, ins):
                splits[0] += 1
                ins.then_inc(hi_done, 1)
                dve.wait_ge(hi_done, b * PER_SPLIT + splits[0])

            def take(b, job):
                wait_filled(dve, b, job)
                bank = ps_g[:, INDEX[job] % 2, :]
                kind, a = job[0], job[1]
                if kind == "ln":
                    n = a
                    return dve.tensor_scalar(h_t[:], bank, W("ln", 2 * n, 2 * n + 1), W("ln", 2 * n + 1, 2 * n + 2),
                                             ALU.mult, ALU.add).then_inc(taken["dve"], 1)
                if kind in ("wo", "y"):
                    n = PHASES.index(("att" if kind == "wo" else "mlp", a))
                    dve.wait_ge(bias_added, b * N_LN + n + 1)
                    dst = xs if (kind, a) != ("y", 1) else y_out
                    return dve.tensor_tensor(dst[:], bank.rearrange("q (t n) -> q t n", t=QT), xs[:],
                                             ALU.add).then_inc(taken["dve"], 1)
                if kind == "lin":
                    m = job[2]
                    wait_taken(dve, b, ("gelu", 1, m))
                    return dve.scalar_tensor_tensor(out=o_t[:, m, :], in0=bank, scalar=W("b1_1", m, m + 1),
                                                    in1=gate[:, m % 2, :], op0=ALU.add,
                                                    op1=ALU.mult).then_inc(taken["dve"], 1)
                layer, own = ATT[a]
                nk = S if own else SK
                s = job[2]
                if kind == "v":
                    if layer == 0:
                        for kt, (_, kn) in enumerate(KT[own]):
                            for j in range(4):
                                last = dve.tensor_tensor(
                                    v0[0:kn, kt, j:H:4, 8 * j:8 * j + 8],
                                    bank[0:kn, 128 * kt:128 * kt + 128].rearrange("k (g j d) -> k j g d", j=4, d=8)[:, j],
                                    W(f"bv{a}", rows=kn).rearrange("k (g j d) -> k j g d", j=4, d=8)[:, j], ALU.add)
                        return last.then_inc(taken["dve"], 1)
                    kt, half = divmod(s, 2)
                    kn = KT[own][kt][1]
                    return dve.tensor_copy(v1[0:kn, kt, 512 * half:512 * half + 512], bank[0:kn, :]).then_inc(
                        taken["dve"], 1)
                if layer == 0:
                    bias = W(f"b{kind}{a}", s, s + 1)
                    if kind == "k" and s >= 2:
                        dve.wait_ge(k_spread[s % 2], b * 256 + 128 * a + 64 * (s // 2))
                    dst = (q0 if kind == "q" else k_parts)[:, s % 2, 0:(S if kind == "q" else nk)]
                    src = bank[:, 0:(S if kind == "q" else nk)]
                    if kind == "q" and s >= 2:
                        unit_wait(dve, scores_ready, b, a, 4 * QT * (s - 1) - 1)
                    split_wait(b, dve.tensor_scalar(dst, src, bias, None, ALU.add))
                    for r, n in ([(64, 64)] if kind == "q" else [(32, 32), (96, 32)]):
                        last = dve.scalar_tensor_tensor(out=dst[r:r + n], in0=src[r:r + n],
                                                        scalar=bias[r:r + n], in1=dst[r:r + n].bitcast(F32),
                                                        op0=ALU.add, op1=ALU.subtract)
                    return last.then_inc(taken["dve"], 1)
                if s >= 2:
                    unit_wait(dve, scores_ready, b, a, QT * (s - 1) - 1)
                if kind == "q":
                    scale = HD[1] ** -0.5
                    split_wait(b, dve.tensor_scalar(q_hi[:, s % 2, :], bank, scale, None, ALU.mult))
                    return dve.scalar_tensor_tensor(out=q_lo[:, s % 2, :], in0=bank, scalar=scale,
                                                    in1=q_hi[:, s % 2, :].bitcast(F32), op0=ALU.mult,
                                                    op1=ALU.subtract).then_inc(taken["dve"], 1)
                dst = k1[:, s % 2, 0:nk]
                split_wait(b, dve.tensor_copy(dst, bank[:, 0:nk]))
                return dve.tensor_tensor(dst[64:128], bank[64:128, 0:nk], dst[64:128].bitcast(F32),
                                         ALU.subtract).then_inc(taken["dve"], 1)

            def layer_norm(b, n):
                src = x_in if n == 0 else xs
                if n == 0:
                    dve.wait_ge(x_loaded, b * 16 + 16)
                else:
                    before = PHASES[n - 1]
                    wait_taken(dve, b, ("wo" if before[0] == "att" else "y", before[1]))
                for t in range(QT):
                    last = dve.bn_stats(stats[:, t, :], src[:, t, :])
                last.then_inc(stats_done, 1)
                dve.wait_ge(stats_done, b * N_LN + n + 1)
                dve.memset(wait_taker[:], 0.0)
                for t in range(QT):
                    last = dve.bn_aggr(mv[:, t, :], stats[:, t, :])
                last.then_inc(mv_done, 1)
                dve.wait_ge(mv_done, b * N_LN + n + 1)
                dve.tensor_scalar(var_eps[:], mv[:, :, 1], EPS, None, ALU.add).then_inc(var_done, 1)
                dve.wait_ge(rstd_done, b * N_LN + n + 1)
                for t in range(QT):
                    last = dve.tensor_scalar(xn[:, t, :], src[:, t, :], mv[:, t, 0:1], rstd[:, t:t + 1],
                                             ALU.subtract, ALU.mult)
                last.then_inc(norm_done, 1)
                take(b, ("ln", n))

            def attention(b, a):
                layer, own = ATT[a]
                nk = S if own else SK
                take(b, ("q", a, 0))
                take(b, ("k", a, 0))
                for job in v_jobs(a):
                    take(b, job)
                for i in range(SLOTS + 1):
                    if i < UNITS:
                        unit_wait(dve, scores_ready, b, a, i)
                        dve.tensor_reduce(neg_max[:, i % 4:i % 4 + 1], ps_s[:, i % NS, 0:nk], AX.X, ALU.max,
                                          negate=True).then_inc(max_ready, 1)
                    u = i - LAG_N
                    if 0 <= u < UNITS:
                        c = slice(u % 4, u % 4 + 1)
                        unit_wait(dve, exp_ready, b, a, u)
                        dve.reciprocal(r_sum[:, c], row_sum[:, c]).then_inc(recip_done, 1)
                        unit_wait(dve, recip_done, b, a, u)
                        dve.tensor_scalar(p[:, u % NP, 0:nk], p[:, u % NP, 0:nk], r_sum[:, c], None,
                                          ALU.mult).then_inc(probs_ready, 1)
                    for job in slot_jobs(a, i):
                        take(b, job)
                    heads = heads_at(a, i)
                    if heads and out_set(a, heads[-1])[1]:
                        o_set = out_set(a, heads[-1])[0]
                        rows = 128 if layer == 1 else 32 * len(KT[own])
                        dve.wait_ge(o_filled, b * PER_O + o_base(a) + o_set + 1)
                        dve.tensor_copy(o_t[0:rows, o_set, :], ps_o[0:rows, :]).then_inc(o_copied, 1)
                take(b, ("wo", a))

            def mlp(b, a):
                if a == 1:
                    for m in range(4):
                        take(b, ("lin", 1, m))
                take(b, ("y", a))

            dve.memset(k0[:].bitcast(F32), 0.0).then_inc(zeros_done, 1)
            dve.memset(v0[:], 0.0).then_inc(zeros_done, 1)
            dve.memset(p_tx[:], 0.0).then_inc(zeros_done, 1)
            for part in range(len(PARTS)):
                dve.wait_ge(w_loaded[part], 16)
            for a in range(2):
                dve.tensor_scalar(W(f"wq{a}"), W(f"wq{a}"), HD[0] ** -0.5, None, ALU.mult).then_inc(scale_done, 1)
                dve.tensor_scalar(W(f"bq{a}"), W(f"bq{a}"), HD[0] ** -0.5, None, ALU.mult).then_inc(scale_done, 1)
            dve.wait_ge(scale_done, 4)
            dve.wait_ge(zeros_done, 3)
            with dve.Fori(0, B) as b:
                for n, (kind, a) in enumerate(PHASES):
                    layer_norm(b, n)
                    (attention if kind == "att" else mlp)(b, a)
            assert splits[0] == PER_SPLIT


def kernel(**inputs):
    import numpy as np
    import concourse.bacc as bacc
    from concourse.bass_utils import run_bass_kernel_spmd

    f = {name: np.asarray(a) for name, a in inputs.items()}

    def full(a):
        return np.concatenate([a, np.zeros((128 - a.shape[0], a.shape[1]), a.dtype)]) if a.shape[0] < 128 else a

    def by_head(wt):
        v = wt.reshape(wt.shape[0], 4, 1, 4, 8).transpose(0, 1, 2, 4, 3)
        return np.broadcast_to(v, (wt.shape[0], 4, 4, 8, 4)).reshape(wt.shape[0], 512)

    def rows(v):
        return np.broadcast_to(v[None, :], (128, v.shape[0]))

    def cols(v):
        return v.reshape(-1, 128).T

    img = {}
    lns = ["L0_xattn_ln1", "L0_xattn_ln2", "L0_xattn_ln3"]
    pairs = [(f[n + "_g"], f[n + "_b"]) for n in lns] + [(f[f"L1_xattn_g{n}"], f[f"L1_xattn_b{n}"]) for n in (1, 2, 3)]
    img["ln"] = np.stack([v for pair in pairs for v in pair], axis=1)
    for a, pre in enumerate(("L0_xattn_sa_", "L0_xattn_ca_")):
        for k in "qk":
            img[f"w{k}{a}"] = full(by_head(f[pre + "w" + k].T))
            img[f"b{k}{a}"] = by_head(f[pre + "b" + k][None, :]).reshape(4, 128).T
        img[f"wv{a}"] = full(f[pre + "wv"].T)
        img[f"bv{a}"] = rows(f[pre + "bv"])
        wo = np.broadcast_to(f[pre + "wo"].T.reshape(4, 1, 32, 128), (4, 4, 32, 128)).reshape(4, 128, 128)
        img[f"wo{a}"] = wo.transpose(1, 0, 2).reshape(128, 512)
        img[f"bo{a}"] = rows(f[pre + "bo"])
    img["w1_0"] = f["L0_xattn_mlp_w1"].T
    img["b1_0"] = cols(f["L0_xattn_mlp_b1"])
    img["w2_0"] = f["L0_xattn_mlp_w2"].T.reshape(4, 128, 128).transpose(1, 0, 2).reshape(128, 512)
    img["b2_0"] = rows(f["L0_xattn_mlp_b2"])
    for a, n in ((2, 1), (3, 2)):
        for k in "qkv":
            img[f"w{k}{a}"] = full(f[f"L1_xattn_W{k}{n}"])
        img[f"wo{a}"] = f[f"L1_xattn_Wo{n}"].reshape(8, 128, 128).transpose(1, 0, 2).reshape(128, 1024)
        img[f"bo{a}"] = rows(f[f"L1_xattn_bo{n}"])
    img["w1_1"] = f["L1_xattn_Wp"]
    img["b1_1"] = cols(f["L1_xattn_bp"])
    img["w2_1"] = f["L1_xattn_Wf"].reshape(4, 128, 128).transpose(1, 0, 2).reshape(128, 512)
    img["b2_1"] = rows(f["L1_xattn_bf"])
    wimg = np.ascontiguousarray(np.concatenate([img[name] for name, _ in FIELDS], axis=1))
    arrays = {
        "x_dram": np.ascontiguousarray(np.concatenate([f["x"], f["x"][:1]])),
        "ctx_t_dram": np.ascontiguousarray(np.concatenate([f["ctx_768"], f["ctx_768"][:1]]).transpose(0, 2, 1)),
        "wimg_dram": wimg,
    }
    nc = bacc.Bacc("TRN2", target_bir_lowering=False, num_devices=1)
    args = [nc.dram_tensor(name, a.shape, mybir.dt.from_np(a.dtype), kind="ExternalInput").ap()
            for name, a in arrays.items()]
    out = nc.dram_tensor("out_dram", (B, S, D), F32, kind="ExternalOutput").ap()
    build(nc, *args, out)
    r = run_bass_kernel_spmd(nc, [arrays], core_ids=[0])
    return r.results[0]["out_dram"]
```

```python
from contextlib import ExitStack

import concourse.bass as bass
from concourse import mybir

F32 = mybir.dt.float32
F32R = mybir.dt.float32r
ALU = mybir.AluOpType
ACT = mybir.ActivationFunctionType
AX = mybir.AxisListType

B, S, D = 4, 512, 128
SK, C = 154, 96
H = 16
HD = (8, 64)
INNER = H * HD[1]
F = 512
QT = S // 128
EPS = 1e-5
KT = {True: [(0, 128), (128, 128), (256, 128), (384, 128)], False: [(0, 128), (128, SK - 128)]}
ATT = [(0, True), (0, False), (1, True), (1, False)]
PHASES = [("att", 0), ("att", 1), ("mlp", 0), ("att", 2), ("att", 3), ("mlp", 1)]
TU = {True: 1, False: 2}

FIELDS = [
    ("ln", 12),
    ("wq0", 512), ("bq0", 4), ("wk0", 512), ("bk0", 4), ("wv0", 128), ("bv0", 128), ("wo0", 512), ("bo0", 128),
    ("wq1", 512), ("bq1", 4), ("wk1", 512), ("bk1", 4), ("wv1", 128), ("bv1", 128), ("wo1", 512), ("bo1", 128),
    ("w1_0", 512), ("b1_0", 4), ("w2_0", 512), ("b2_0", 128),
    ("wq2", INNER), ("wk2", INNER), ("wv2", INNER), ("wo2", INNER), ("bo2", 128),
    ("wq3", INNER), ("wk3", INNER), ("wv3", INNER), ("wo3", INNER), ("bo3", 128),
    ("w1_1", 2 * F), ("b1_1", 8), ("w2_1", 512), ("b2_1", 128),
]
AT, _at = {}, 0
for _name, _w in FIELDS:
    AT[_name] = (_at, _at + _w)
    _at += _w
WCOLS = _at
PARTS = [("ln", "wq1"), ("wq1", "w1_0"), ("w1_0", "wq2"), ("wq2", "wq3"), ("wq3", "w1_1"), ("w1_1", None)]
PART_OF_PHASE = {("att", 0): 0, ("att", 1): 1, ("mlp", 0): 2, ("att", 2): 3, ("att", 3): 4, ("mlp", 1): 5}


def steps(a):
    return 4 if ATT[a][0] == 0 else 8


def tiles_of(a):
    return TU[ATT[a][1]]


def units(a):
    return H * QT // tiles_of(a)


def v_jobs(a):
    layer, own = ATT[a]
    if layer == 0:
        return [("v", a, 0)]
    return [("v", a, 2 * n + half) for n in range(len(KT[own])) for half in range(2)]


def plan():
    jobs, bank, before = [], {}, {}
    last = {}

    def add(job, eng, own_bank):
        side = 0 if own_bank or last.get("side") == 1 else 1
        last["side"] = side
        jobs.append((job, eng))
        bank[job] = side
        before[job] = last.get(side)
        last[side] = job

    for n, (kind, a) in enumerate(PHASES):
        add(("ln", n), "dve", False)
        if kind == "att":
            add(("q", a, 0), "dve", False)
            add(("k", a, 0), "dve", False)
            for n, j in enumerate(v_jobs(a)):
                add(j, "act" if ATT[a][0] == 1 and n % 2 == 0 else "dve", False)
            for s in range(1, steps(a)):
                add(("q", a, s), "dve", True)
                add(("k", a, s), "dve", True)
        else:
            for m in range(4):
                add(("gelu", a, m), "act", False)
                if a == 1:
                    add(("lin", a, m), "dve", False)
    index, count, per = {}, {}, {"dve": 0, "act": 0}
    for n, (job, eng) in enumerate(jobs):
        per[eng] += 1
        index[job], count[job] = n, per[eng]
    return jobs, index, count, per, bank, before


JOBS, INDEX, TAKEN, PER, BANK, BEFORE = plan()


def build(nc, x, ctx_t, wimg, out):
    with ExitStack() as ctx:
        def sb(name, shape, dt=F32):
            return ctx.enter_context(nc.sbuf_tensor(name, shape, dt))

        def psum(name, shape):
            return ctx.enter_context(nc.psum_tensor(name, shape, F32))

        def sem(name):
            return ctx.enter_context(nc.semaphore(name))

        w = sb("w", [128, WCOLS])
        ident = sb("ident", [128, 128])
        x_in = sb("x_in", [128, QT, D])
        xs = sb("xs", [128, QT, D])
        y_out = sb("y_out", [128, QT, D])
        c_t = sb("c_t", [C, SK])
        xn = sb("xn", [128, QT, D])
        stats = sb("stats", [128, QT, 6])
        mv = sb("mv", [128, QT, 2])
        var_eps = sb("var_eps", [128, QT])
        minus_half = sb("minus_half", [128, QT])
        rstd = sb("rstd", [128, QT])
        wait_taker = sb("wait_taker", [128, 1])
        h_t = sb("h_t", [128, S])
        q_parts = sb("q_parts", [128, 2, S], F32R)
        k_parts = sb("k_parts", [128, 2, S], F32R)
        k0 = sb("k0", [128, 2, 4, S], F32R)
        v0 = sb("v0", [128, 4, H, 32])
        q1 = sb("q1", [128, 2, 2, 2, S], F32R)
        k1 = sb("k1", [128, 2, 2, S], F32R)
        v1 = sb("v1", [128, 4, INNER])
        NP, NPT, NR = 5, 4, 8
        p = sb("p", [128, NP, S])
        p_t = sb("p_t", [128, NPT, 4, S])
        neg_max = sb("neg_max", [128, NR, 2])
        row_sum = sb("row_sum", [128, NR, 2])
        r_sum = sb("r_sum", [128, NR, 2])
        o_t = sb("o_t", [128, 4, S])

        NS, NT = 3, 2
        ps_s = psum("ps_s", [128, NS, 512])
        ps_t = psum("ps_t", [128, NT, 512])
        ps_g = psum("ps_g", [128, 512])
        ps_o = psum("ps_o", [128, 512])
        ps_y = psum("ps_y", [128, 512])

        w_loaded = [sem(f"w_loaded{n}") for n in range(len(PARTS))]
        x_loaded = sem("x_loaded")
        c_loaded = sem("c_loaded")
        ident_done = sem("ident_done")
        zeros_done = sem("zeros_done")
        scale_done = sem("scale_done")
        out_stored = sem("out_stored")
        stats_done = sem("stats_done")
        mv_done = sem("mv_done")
        var_done = sem("var_done")
        rstd_done = sem("rstd_done")
        norm_done = sem("norm_done")
        bias_added = sem("bias_added")
        gen_filled = sem("gen_filled")
        taken = {"dve": sem("taken_by_dve"), "act": sem("taken_by_act")}
        hi_done = sem("hi_done")
        k_spread = [sem("k_spread0"), sem("k_spread1")]
        q_moved = [sem("q_moved0"), sem("q_moved1")]
        k_moved = [sem("k_moved0"), sem("k_moved1")]
        p_t_zeroed = sem("p_t_zeroed")
        y_filled = sem("y_filled")
        residual_done = sem("residual_done")
        scores_ready = sem("scores_ready")
        max_ready = sem("max_ready")
        exp_ready = sem("exp_ready")
        recip_done = sem("recip_done")
        probs_ready = sem("probs_ready")
        pt_filled = sem("pt_filled")
        pt_copied = sem("pt_copied")
        o_filled = sem("o_filled")
        o_copied = sem("o_copied")

        def bank_of(job):
            return ps_o[:] if BANK[job] else ps_g[:]

        def W(name, lo=0, hi=None, rows=128):
            a, z = AT[name]
            return w[0:rows, a + lo:(z if hi is None else a + hi)]

        PER_HI = sum(2 * steps(a) for a in range(4))
        PER_O = sum(steps(a) for a in range(4))
        PER_UNIT = sum(units(a) for a in range(4))
        N_LN = len(PHASES)
        PER_SPREAD = 2 * 2 * 64
        PER_MOVED = 2 * 4 * 64

        def o_base(a):
            return sum(steps(n) for n in range(a))

        def wait_taken(eng, b, job):
            who = dict(JOBS)[job]
            eng.wait_ge(taken[who], b * PER[who] + TAKEN[job])

        def wait_filled(eng, b, job):
            eng.wait_ge(gen_filled, b * len(JOBS) + INDEX[job] + 1)

        def wait_hi(eng, b, job):
            kind, a, s = job
            eng.wait_ge(hi_done, b * PER_HI + 2 * (o_base(a) + s) + (1 if kind == "q" else 2))

        def wait_moved(eng, moved, b, a, s):
            per = PER_MOVED if moved is q_moved else PER_MOVED // 2
            eng.wait_ge(moved[s % 2], b * per + (a - 2) * 256 + 64 * (s // 2 + 1))

        def wait_spread(eng, b, a, s):
            eng.wait_ge(k_spread[s % 2], b * PER_SPREAD + a * 128 + 64 * (s // 2 + 1))

        def unit_wait(eng, semaphore, b, a, i):
            eng.wait_ge(semaphore, b * PER_UNIT + sum(units(n) for n in range(a)) + i + 1)

        LAG_E, LAG_N, LAG_T, LAG_C = 1, 2, 4, 5

        def per_step(a):
            return units(a) // steps(a)

        def per_head(a):
            return QT // tiles_of(a)

        def slots(a):
            return units(a) + LAG_C + per_step(a) + QT

        def jobs_at(a, i, q_at, k_at):
            for s in range(1, steps(a)):
                if per_step(a) * (s - 1) + q_at == i:
                    yield ("q", a, s)
                if per_step(a) * (s - 1) + k_at == i:
                    yield ("k", a, s)

        def values_at(a, i):
            tiles = len(KT[ATT[a][1]])
            heads = 1 if ATT[a][0] == 0 else 2
            span = heads * per_head(a)
            n, r = (i - LAG_C) // span - 1, (i - LAG_C) % span
            return [(heads * n * steps(a) // H, list(range(heads * n, heads * n + heads)), kt)
                    for kt in range(tiles) if 0 <= heads * n < H and kt * span // tiles == r]

        def after_values(a):
            return LAG_C + per_head(a) * (1 if ATT[a][0] == 0 else 2)

        def copy_at(a, i):
            i -= after_values(a) - 1
            s = i // per_step(a) - 1
            return s if i % per_step(a) == 0 and 0 <= s < steps(a) else None

        def result_at(a, i):
            i -= after_values(a)
            s, t = i // per_step(a) - 1, i % per_step(a)
            return (s, t) if t < QT and 0 <= s < steps(a) else None

        block = ctx.enter_context(nc.Block())

        @block.sync
        def _(sp):
            for n, (first, end) in enumerate(PARTS):
                lo, hi = AT[first][0], (AT[end][0] if end else WCOLS)
                sp.dma_start(w[:, lo:hi], wimg[:, lo:hi]).then_inc(w_loaded[n], 16)
            with sp.Fori(0, B) as b:
                for a in range(2):
                    for g in range(4):
                        wait_taken(sp, b, ("k", a, g))
                        for j in range(4):
                            nk = S if ATT[a][1] else SK
                            sp.dma_start(k0[j:128:4, g % 2, j, 0:nk].bitcast(F32),
                                         k_parts[j:128:4, g % 2, 0:nk].bitcast(F32)).then_inc(k_spread[g % 2], 16)
                for a in (2, 3):
                    nk = S if ATT[a][1] else SK
                    for s in range(steps(a)):
                        wait_taken(sp, b, ("q", a, s))
                        for e in range(2):
                            for r in (0, 64):
                                sp.dma_start(q1[r:r + 64, s % 2, e].bitcast(F32),
                                             q_parts[64 * e:64 * e + 64].bitcast(F32)).then_inc(q_moved[s % 2], 16)
                        if a == 3:
                            continue
                        wait_taken(sp, b, ("k", a, s))
                        for e in range(2):
                            for part in range(2):
                                sp.dma_start(k1[64 * part:64 * part + 64, s % 2, e, 0:nk].bitcast(F32),
                                             k_parts[64 * e:64 * e + 64, part, 0:nk].bitcast(F32)).then_inc(
                                                 k_moved[s % 2], 16)

        @block.gpsimd
        def _(pool):
            pool.dma_start(x_in[:], x[0].rearrange("(t p) d -> p t d", p=128)).then_inc(x_loaded, 16)
            pool.dma_start(c_t[:], ctx_t[0]).then_inc(c_loaded, 16)
            pool.memset(minus_half[:], -0.5).then_inc(ident_done, 1)
            pool.memset(ident[:], 0.0).then_inc(ident_done, 1)
            pool.wait_ge(ident_done, 2)
            pool.affine_select(out=ident[:], in_=ident[:], compare_op=ALU.not_equal, fill=1.0, base=0,
                               pattern=[[-1, 128]], channel_multiplier=1).then_inc(ident_done, 1)
            with pool.Fori(0, B) as b:
                for n, (kind, a) in enumerate(PHASES):
                    pool.wait_ge(var_done, b * N_LN + n + 1)
                    pool.tensor_tensor(rstd[:], var_eps[:], minus_half[:], ALU.pow).then_inc(rstd_done, 1)
                    if (kind, a) in (("att", 1), ("att", 3)):
                        pool.memset(p_t[:, :, 1, :], 0.0).then_inc(p_t_zeroed, 1)
                    pool.wait_ge(norm_done, b * N_LN + n + 1)
                    if n == 0:
                        pool.wait_ge(w_loaded[5], 16)
                        for part in range(5):
                            pool.wait_ge(w_loaded[part], 16)
                    bias = W(f"bo{a}") if kind == "att" else W(f"b2_{a}")
                    pool.tensor_tensor(xs[:], x_in[:] if n == 0 else xs[:],
                                       bias[:, None, :].to_broadcast([128, QT, D]), ALU.add).then_inc(bias_added, 1)
                    if n == 0:
                        pool.wait_ge(bias_added, b * N_LN + 1)
                        pool.dma_start(x_in[:], x[1:B + 1][b].rearrange("(t p) d -> p t d", p=128)).then_inc(x_loaded, 16)

                    if n == 4:
                        wait_taken(pool, b, ("k", 3, 7))
                        pool.dma_start(c_t[:], ctx_t[1:B + 1][b]).then_inc(c_loaded, 16)
                pool.wait_ge(residual_done, b * N_LN + N_LN)
                pool.dma_start(out[b].rearrange("(t p) d -> p t d", p=128), y_out[:]).then_inc(out_stored, 16)
                pool.wait_ge(out_stored, b * 16 + 16)
            pool.wait_ge(out_stored, 16 * B)
            pool.wait_ge(x_loaded, 16 * (B + 1))
            pool.wait_ge(c_loaded, 16 * (B + 1))

        @block.tensor
        def _(pe):
            def product(b, job, emit):
                if BEFORE[job]:
                    wait_taken(pe, b, BEFORE[job])
                emit(bank_of(job)).then_inc(gen_filled, 1)

            def transposes(n):
                def emit(bank):
                    for t in range(QT):
                        last = pe.transpose(bank[:, 128 * t:128 * t + 128], xn[:, t, :], ident[:])
                    return last
                return emit

            def qk_product(kind, a, s):
                if kind == "q" or ATT[a][1]:
                    rows, src, nk = 128, h_t[:], S
                else:
                    rows, src, nk = C, c_t[:], SK
                if a == 3 and kind == "k":
                    def emit(bank):
                        for e in range(2):
                            for r in (0, 64):
                                last = pe.matmul(bank[r:r + 64, nk * e:nk * e + nk],
                                                 W("wk3", 64 * (2 * s + e), 64 * (2 * s + e) + 64, rows), src,
                                                 start=True, stop=True)
                        return last
                    return emit
                return lambda bank: pe.matmul(bank[:, 0:nk], W(f"w{kind}{a}", 128 * s, 128 * s + 128, rows), src,
                                              start=True, stop=True)

            def v_product(a, n):
                layer, own = ATT[a]
                rows, src = (128, h_t) if own else (C, c_t)

                def emit(bank):
                    if layer == 0:
                        for kt, (k0_, kn) in enumerate(KT[own]):
                            last = pe.matmul(bank[0:kn, 128 * kt:128 * kt + 128], src[:, k0_:k0_ + kn],
                                             W(f"wv{a}", rows=rows), start=True, stop=True)
                        return last
                    k0_, kn = KT[own][n // 2]
                    half = n % 2
                    return pe.matmul(bank[0:kn, :], src[:, k0_:k0_ + kn],
                                     W(f"wv{a}", 512 * half, 512 * half + 512, rows), start=True, stop=True)
                return emit

            def step_product(b, job):
                kind, a, s = job
                product(b, job, qk_product(kind, a, s))

            def result(hidden, weights, rows, t, first, last):
                return pe.matmul(ps_y[:, 128 * t:128 * t + 128], hidden[0:rows, 128 * t:128 * t + 128], weights,
                                 start=first and t == 0, stop=last, skip_group_check=True)

            def attention(b, n, a):
                layer, own = ATT[a]
                nk = S if own else SK
                tiles, tu = len(KT[own]), TU[own]
                rows = 128 if layer == 1 else 32 * tiles
                if not own and layer == 0:
                    pe.wait_ge(c_loaded, b * 16 + 16)
                wait_taken(pe, b, ("ln", n))
                step_product(b, ("q", a, 0))
                step_product(b, ("k", a, 0))
                for job in v_jobs(a):
                    product(b, job, v_product(a, job[2]))
                for i in range(slots(a)):
                    if i < units(a):
                        h, n = divmod(i, per_head(a))
                        s = i // per_step(a)
                        if i % per_step(a) == 0:
                            if layer == 0:
                                wait_taken(pe, b, ("q", a, s))
                                wait_spread(pe, b, a, s)
                            else:
                                wait_moved(pe, q_moved, b, a, s)
                                if own:
                                    wait_moved(pe, k_moved, b, a, s)
                                else:
                                    wait_taken(pe, b, ("k", a, s))
                        if i >= NS:
                            unit_wait(pe, exp_ready, b, a, i - NS)
                        for t in range(tu):
                            bank = ps_s[:, i % NS, nk * t:nk * t + nk]
                            cols = slice(128 * (n * tu + t), 128 * (n * tu + t) + 128)
                            if layer == 0:
                                last = pe.matmul(bank, q_parts[:, s % 2, cols], k0[:, s % 2, h % 4, 0:nk],
                                                 start=True, stop=True)
                            else:
                                for part in range(2):
                                    last = pe.matmul(bank, q1[:, s % 2, h % 2, part, cols], k1[:, s % 2, h % 2, 0:nk],
                                                     start=part == 0, stop=part == 1)
                        last.then_inc(scores_ready, 1)
                    for job in jobs_at(a, i, 0, 2):
                        step_product(b, job)
                    for s, heads, kt in values_at(a, i):
                        first = kt == 0 and (layer == 1 or heads[0] % 4 == 0)
                        full = kt == tiles - 1 and (layer == 1 or heads[0] % 4 == 3)
                        if kt == 0:
                            unit_wait(pe, pt_copied, b, a, per_head(a) * (heads[-1] + 1) - 1)
                            if heads[0] == 0:
                                for job in v_jobs(a)[-2:]:
                                    wait_taken(pe, b, job)
                                if not own:
                                    pe.wait_ge(p_t_zeroed, b * 2 + layer + 1)
                        if first and s > 0:
                            pe.wait_ge(o_copied, b * PER_O + o_base(a) + s)
                        for h in heads:
                            if layer == 0:
                                last = pe.matmul(ps_o[32 * kt:32 * kt + 32, :], v0[:, kt, h, :], p_t[:, h % NPT, kt, :],
                                                 start=h % 4 == 0, stop=h % 4 == 3, skip_group_check=True)
                            else:
                                r = 64 * (h % 2)
                                last = pe.matmul(ps_o[r:r + 64, :], v1[:, kt, 64 * h:64 * h + 64],
                                                 p_t[:, h % NPT, kt, :], start=kt == 0, stop=kt == tiles - 1)
                        if full:
                            last.then_inc(o_filled, 1)
                    u = i - LAG_T
                    if 0 <= u < units(a):
                        unit_wait(pe, probs_ready, b, a, u)
                        if u >= NT:
                            unit_wait(pe, pt_copied, b, a, u - NT)
                        for kt, (k0_, kn) in enumerate(KT[own]):
                            for t in range(tu):
                                at = 128 * (kt * tu + t)
                                last = pe.transpose(ps_t[0:kn, u % NT, at:at + 128],
                                                    p[:, u % NP, nk * t + k0_:nk * t + k0_ + kn], ident[:])
                        last.then_inc(pt_filled, 1)
                    r = result_at(a, i)
                    if r:
                        s, t = r
                        if t == 0:
                            pe.wait_ge(o_copied, b * PER_O + o_base(a) + s + 1)
                        end = s == steps(a) - 1
                        last = result(o_t[:, s % 2], W(f"wo{a}", 128 * s, 128 * s + 128, rows), rows, t, s == 0, end)
                        if end and t == QT - 1:
                            last.then_inc(y_filled, 1)

            def mlp(b, n, a):
                wait_taken(pe, b, ("ln", n))

                def hidden(m):
                    off = F if a == 1 else 0
                    product(b, ("gelu", a, m), lambda bank: pe.matmul(
                        bank, W(f"w1_{a}", off + 128 * m, off + 128 * m + 128), h_t[:], start=True, stop=True))
                    if a == 1:
                        product(b, ("lin", a, m), lambda bank: pe.matmul(
                            bank, W(f"w1_{a}", 128 * m, 128 * m + 128), h_t[:], start=True, stop=True))

                def output(m):
                    wait_taken(pe, b, ("gelu", 0, m) if a == 0 else ("lin", 1, m))
                    for t in range(QT):
                        last = result(o_t[:, m], W(f"w2_{a}", 128 * m, 128 * m + 128), 128, t, m == 0, m == 3)
                    if m == 3:
                        last.then_inc(y_filled, 1)

                hidden(0)
                for m in range(1, 4):
                    hidden(m)
                    output(m - 1)
                output(3)

            pe.wait_ge(ident_done, 3)
            for part in range(len(PARTS)):
                pe.wait_ge(w_loaded[part], 16)
            pe.wait_ge(scale_done, 4)
            pe.wait_ge(zeros_done, 2)
            with pe.Fori(0, B) as b:
                for n, (kind, a) in enumerate(PHASES):
                    pe.wait_ge(norm_done, b * N_LN + n + 1)
                    product(b, ("ln", n), transposes(n))
                    (attention if kind == "att" else mlp)(b, n, a)

        @block.scalar
        def _(act):
            def hi_part(b, job):
                kind, a, s = job
                layer, own = ATT[a]
                nk = S if kind == "q" or own else SK
                wait_filled(act, b, job)
                src = bank_of(job)[:, 0:nk]
                parts = q_parts if kind == "q" else k_parts
                if layer == 0:
                    if s >= 2 and kind == "q":
                        unit_wait(act, scores_ready, b, a, per_step(a) * (s - 1) - 1)
                    if s >= 2 and kind == "k":
                        wait_spread(act, b, a, s - 2)
                    act.activation(parts[:, s % 2, 0:nk], src, ACT.Identity, bias=W(f"b{kind}{a}", s, s + 1),
                                   scale=1.0).then_inc(hi_done, 1)
                elif a == 3 and kind == "k":
                    if s >= 2:
                        unit_wait(act, scores_ready, b, a, per_step(a) * (s - 1) - 1)
                    act.activation(k1[:, s % 2, :, 0:nk], bank_of(job)[:, 0:2 * nk].rearrange("d (e k) -> d e k", e=2),
                                   ACT.Copy).then_inc(hi_done, 1)
                else:
                    if s >= 1:
                        wait_moved(act, q_moved if kind == "q" else k_moved, b, a, s - 1)
                    act.activation(parts[:, 0, 0:nk], src, ACT.Copy,
                                   scale=HD[1] ** -0.5 if kind == "q" else 1.0).then_inc(hi_done, 1)

            def attention(b, a):
                layer, own = ATT[a]
                nk, tu = S if own else SK, TU[own]
                hi_part(b, ("q", a, 0))
                hi_part(b, ("k", a, 0))
                if layer == 1:
                    for job in v_jobs(a)[0::2]:
                        kt, half = divmod(job[2], 2)
                        kn = KT[own][kt][1]
                        wait_filled(act, b, job)
                        act.activation(v1[0:kn, kt, 512 * half:512 * half + 512], bank_of(job)[0:kn, :],
                                       ACT.Copy).then_inc(taken["act"], 1)
                for i in range(slots(a)):
                    u = i - LAG_C
                    if 0 <= u < units(a):
                        h, n = divmod(u, per_head(a))
                        cols = slice(128 * tu * n, 128 * tu * (n + 1))
                        unit_wait(act, pt_filled, b, a, u)
                        if own:
                            act.activation(p_t[:, h % NPT, :, cols],
                                           ps_t[:, u % NT, :].rearrange("k (n q) -> k n q", n=4),
                                           ACT.Copy).then_inc(pt_copied, 1)
                        else:
                            kn = SK - 128
                            if u == 0:
                                act.wait_ge(p_t_zeroed, b * 2 + layer + 1)
                            act.activation(p_t[:, h % NPT, 0, cols], ps_t[:, u % NT, 0:256], ACT.Copy)
                            act.activation(p_t[0:kn, h % NPT, 1, cols], ps_t[0:kn, u % NT, 256:512],
                                           ACT.Copy).then_inc(pt_copied, 1)
                    u = i - LAG_E
                    if 0 <= u < units(a):
                        unit_wait(act, max_ready, b, a, u)
                        if u >= NP:
                            unit_wait(act, pt_filled, b, a, u - NP)
                        for t in range(tu):
                            last = act.activation(p[:, u % NP, nk * t:nk * t + nk], ps_s[:, u % NS, nk * t:nk * t + nk],
                                                  ACT.Exp, bias=neg_max[:, u % NR, t:t + 1], scale=1.0,
                                                  accum_out=row_sum[:, u % NR, t:t + 1])
                        last.then_inc(exp_ready, 1)
                    for job in jobs_at(a, i, 1, 3):
                        hi_part(b, job)

            def mlp(b, a):
                for m in range(4):
                    wait_filled(act, b, ("gelu", a, m))
                    if a == 0:
                        dst = o_t[:, m, :]
                    else:
                        dst = p[:, m % 2, :]
                        if m >= 2:
                            wait_taken(act, b, ("lin", 1, m - 2))
                    bias = W(f"b1_{a}", 4 * a + m, 4 * a + m + 1)
                    act.activation(dst, bank_of(("gelu", a, m)), ACT.Gelu,
                                   bias=bias, scale=1.0).then_inc(taken["act"], 1)

            for part in (2, 5):
                act.wait_ge(w_loaded[part], 16)
            act.wait_ge(zeros_done, 2)
            with act.Fori(0, B) as b:
                for kind, a in PHASES:
                    (attention if kind == "att" else mlp)(b, a)

        @block.vector
        def _(dve):
            def take(b, job):
                wait_filled(dve, b, job)
                bank = bank_of(job)
                kind, a = job[0], job[1]
                if kind == "ln":
                    n = a
                    return dve.tensor_scalar(h_t[:], bank, W("ln", 2 * n, 2 * n + 1), W("ln", 2 * n + 1, 2 * n + 2),
                                             ALU.mult, ALU.add).then_inc(taken["dve"], 1)
                if kind == "lin":
                    m = job[2]
                    wait_taken(dve, b, ("gelu", 1, m))
                    return dve.scalar_tensor_tensor(out=o_t[:, m, :], in0=bank, scalar=W("b1_1", m, m + 1),
                                                    in1=p[:, m % 2, :], op0=ALU.add,
                                                    op1=ALU.mult).then_inc(taken["dve"], 1)
                layer, own = ATT[a]
                nk = S if own else SK
                s = job[2]
                if kind == "v":
                    if layer == 0:
                        for kt, (_, kn) in enumerate(KT[own]):
                            for j in range(4):
                                last = dve.tensor_tensor(
                                    v0[0:kn, kt, j:H:4, 8 * j:8 * j + 8],
                                    bank[0:kn, 128 * kt:128 * kt + 128].rearrange("k (g j d) -> k j g d", j=4, d=8)[:, j],
                                    W(f"bv{a}", rows=kn).rearrange("k (g j d) -> k j g d", j=4, d=8)[:, j], ALU.add)
                        return last.then_inc(taken["dve"], 1)
                    kt, half = divmod(s, 2)
                    kn = KT[own][kt][1]
                    return dve.tensor_copy(v1[0:kn, kt, 512 * half:512 * half + 512], bank[0:kn, :]).then_inc(
                        taken["dve"], 1)
                wait_hi(dve, b, job)
                nk = S if kind == "q" else nk
                src = bank[:, 0:nk]
                parts = q_parts if kind == "q" else k_parts
                if layer == 0:
                    bias = W(f"b{kind}{a}", s, s + 1)
                    dst = parts[:, s % 2, 0:nk]
                    for r, n in ([(64, 64)] if kind == "q" else [(32, 32), (96, 32)]):
                        last = dve.scalar_tensor_tensor(out=dst[r:r + n], in0=src[r:r + n],
                                                        scalar=bias[r:r + n], in1=dst[r:r + n].bitcast(F32),
                                                        op0=ALU.add, op1=ALU.subtract)
                    return last.then_inc(taken["dve"], 1)
                if a == 3 and kind == "k":
                    dst = k1[64:128, s % 2, :, 0:nk]
                    return dve.tensor_tensor(dst, bank[64:128, 0:2 * nk].rearrange("d (e k) -> d e k", e=2),
                                             dst.bitcast(F32), ALU.subtract).then_inc(taken["dve"], 1)
                return dve.scalar_tensor_tensor(out=parts[:, 1, 0:nk], in0=src,
                                                scalar=HD[1] ** -0.5 if kind == "q" else 1.0,
                                                in1=parts[:, 0, 0:nk].bitcast(F32), op0=ALU.mult,
                                                op1=ALU.subtract).then_inc(taken["dve"], 1)

            def residual(b, n):
                dve.wait_ge(y_filled, b * N_LN + n + 1)
                dve.wait_ge(bias_added, b * N_LN + n + 1)
                dst = xs if n < N_LN - 1 else y_out
                dve.tensor_tensor(dst[:], ps_y[:].rearrange("q (t n) -> q t n", t=QT), xs[:],
                                  ALU.add).then_inc(residual_done, 1)

            def layer_norm(b, n):
                src = x_in if n == 0 else xs
                if n == 0:
                    dve.wait_ge(x_loaded, b * 16 + 16)
                else:
                    dve.wait_ge(residual_done, b * N_LN + n)
                for t in range(QT):
                    last = dve.bn_stats(stats[:, t, :], src[:, t, :])
                last.then_inc(stats_done, 1)
                dve.wait_ge(stats_done, b * N_LN + n + 1)
                dve.memset(wait_taker[:], 0.0)
                for t in range(QT):
                    last = dve.bn_aggr(mv[:, t, :], stats[:, t, :])
                last.then_inc(mv_done, 1)
                dve.wait_ge(mv_done, b * N_LN + n + 1)
                dve.tensor_scalar(var_eps[:], mv[:, :, 1], EPS, None, ALU.add).then_inc(var_done, 1)
                dve.wait_ge(rstd_done, b * N_LN + n + 1)
                for t in range(QT):
                    last = dve.tensor_scalar(xn[:, t, :], src[:, t, :], mv[:, t, 0:1], rstd[:, t:t + 1],
                                             ALU.subtract, ALU.mult)
                last.then_inc(norm_done, 1)
                take(b, ("ln", n))

            def attention(b, a):
                layer, own = ATT[a]
                nk, tu = S if own else SK, TU[own]
                take(b, ("q", a, 0))
                take(b, ("k", a, 0))
                for job in v_jobs(a)[layer::layer + 1]:
                    take(b, job)
                for i in range(slots(a)):
                    if i < units(a):
                        unit_wait(dve, scores_ready, b, a, i)
                        dve.tensor_reduce(neg_max[:, i % NR, 0:tu],
                                          ps_s[:, i % NS, 0:tu * nk].rearrange("q (t k) -> q t k", t=tu),
                                          AX.X, ALU.max, negate=True).then_inc(max_ready, 1)
                    u = i - LAG_N
                    if 0 <= u < units(a):
                        unit_wait(dve, exp_ready, b, a, u)
                        dve.reciprocal(r_sum[:, u % NR, 0:tu], row_sum[:, u % NR, 0:tu]).then_inc(recip_done, 1)
                        unit_wait(dve, recip_done, b, a, u)
                        for t in range(tu):
                            part = p[:, u % NP, nk * t:nk * t + nk]
                            last = dve.tensor_scalar(part, part, r_sum[:, u % NR, t:t + 1], None, ALU.mult)
                        last.then_inc(probs_ready, 1)
                    for job in jobs_at(a, i, 1, 3):
                        take(b, job)
                    s = copy_at(a, i)
                    if s is not None:
                        rows = 128 if layer == 1 else 32 * len(KT[own])
                        dve.wait_ge(o_filled, b * PER_O + o_base(a) + s + 1)
                        dve.tensor_copy(o_t[0:rows, s % 2, :], ps_o[0:rows, :]).then_inc(o_copied, 1)

            def mlp(b, a):
                if a == 1:
                    for m in range(4):
                        take(b, ("lin", 1, m))

            dve.memset(k0[:].bitcast(F32), 0.0).then_inc(zeros_done, 1)
            dve.memset(v0[:], 0.0).then_inc(zeros_done, 1)
            for part in range(len(PARTS)):
                dve.wait_ge(w_loaded[part], 16)
            for a in range(2):
                dve.tensor_scalar(W(f"wq{a}"), W(f"wq{a}"), HD[0] ** -0.5, None, ALU.mult).then_inc(scale_done, 1)
                dve.tensor_scalar(W(f"bq{a}"), W(f"bq{a}"), HD[0] ** -0.5, None, ALU.mult).then_inc(scale_done, 1)
            dve.wait_ge(scale_done, 4)
            dve.wait_ge(zeros_done, 2)
            with dve.Fori(0, B) as b:
                for n, (kind, a) in enumerate(PHASES):
                    layer_norm(b, n)
                    (attention if kind == "att" else mlp)(b, a)
                    residual(b, n)


def kernel(**inputs):
    import numpy as np
    import concourse.bacc as bacc
    from concourse.bass_utils import run_bass_kernel_spmd

    f = {name: np.asarray(a) for name, a in inputs.items()}

    def full(a):
        return np.concatenate([a, np.zeros((128 - a.shape[0], a.shape[1]), a.dtype)]) if a.shape[0] < 128 else a

    def by_head(wt):
        v = wt.reshape(wt.shape[0], 4, 1, 4, 8).transpose(0, 1, 2, 4, 3)
        return np.broadcast_to(v, (wt.shape[0], 4, 4, 8, 4)).reshape(wt.shape[0], 512)

    def rows(v):
        return np.broadcast_to(v[None, :], (128, v.shape[0]))

    def cols(v):
        return v.reshape(-1, 128).T

    img = {}
    lns = ["L0_xattn_ln1", "L0_xattn_ln2", "L0_xattn_ln3"]
    pairs = [(f[n + "_g"], f[n + "_b"]) for n in lns] + [(f[f"L1_xattn_g{n}"], f[f"L1_xattn_b{n}"]) for n in (1, 2, 3)]
    img["ln"] = np.stack([v for pair in pairs for v in pair], axis=1)
    for a, pre in enumerate(("L0_xattn_sa_", "L0_xattn_ca_")):
        for k in "qk":
            img[f"w{k}{a}"] = full(by_head(f[pre + "w" + k].T))
            img[f"b{k}{a}"] = by_head(f[pre + "b" + k][None, :]).reshape(4, 128).T
        img[f"wv{a}"] = full(f[pre + "wv"].T)
        img[f"bv{a}"] = rows(f[pre + "bv"])
        wo = np.broadcast_to(f[pre + "wo"].T.reshape(4, 1, 32, 128), (4, 4, 32, 128)).reshape(4, 128, 128)
        img[f"wo{a}"] = wo.transpose(1, 0, 2).reshape(128, 512)
        img[f"bo{a}"] = rows(f[pre + "bo"])
    img["w1_0"] = f["L0_xattn_mlp_w1"].T
    img["b1_0"] = cols(f["L0_xattn_mlp_b1"])
    img["w2_0"] = f["L0_xattn_mlp_w2"].T.reshape(4, 128, 128).transpose(1, 0, 2).reshape(128, 512)
    img["b2_0"] = rows(f["L0_xattn_mlp_b2"])
    for a, n in ((2, 1), (3, 2)):
        for k in "qkv":
            img[f"w{k}{a}"] = full(f[f"L1_xattn_W{k}{n}"])
        img[f"wo{a}"] = f[f"L1_xattn_Wo{n}"].reshape(8, 128, 128).transpose(1, 0, 2).reshape(128, 1024)
        img[f"bo{a}"] = rows(f[f"L1_xattn_bo{n}"])
    img["w1_1"] = f["L1_xattn_Wp"]
    img["b1_1"] = cols(f["L1_xattn_bp"])
    img["w2_1"] = f["L1_xattn_Wf"].reshape(4, 128, 128).transpose(1, 0, 2).reshape(128, 512)
    img["b2_1"] = rows(f["L1_xattn_bf"])
    wimg = np.ascontiguousarray(np.concatenate([img[name] for name, _ in FIELDS], axis=1))
    arrays = {
        "x_dram": np.ascontiguousarray(np.concatenate([f["x"], f["x"][:1]])),
        "ctx_t_dram": np.ascontiguousarray(np.concatenate([f["ctx_768"], f["ctx_768"][:1]]).transpose(0, 2, 1)),
        "wimg_dram": wimg,
    }
    nc = bacc.Bacc("TRN2", target_bir_lowering=False, num_devices=1)
    args = [nc.dram_tensor(name, a.shape, mybir.dt.from_np(a.dtype), kind="ExternalInput").ap()
            for name, a in arrays.items()]
    out = nc.dram_tensor("out_dram", (B, S, D), F32, kind="ExternalOutput").ap()
    build(nc, *args, out)
    r = run_bass_kernel_spmd(nc, [arrays], core_ids=[0])
    return r.results[0]["out_dram"]
```

```python
from contextlib import ExitStack

import concourse.bass as bass
from concourse import mybir

F32 = mybir.dt.float32
F32R = mybir.dt.float32r
ALU = mybir.AluOpType
ACT = mybir.ActivationFunctionType
AX = mybir.AxisListType

B, S, D = 4, 512, 128
SK, C = 154, 96
H = 16
HD = (8, 64)
INNER = H * HD[1]
F = 512
QT = S // 128
EPS = 1e-5
KT = {True: [(0, 128), (128, 128), (256, 128), (384, 128)], False: [(0, 128), (128, SK - 128)]}
ATT = [(0, True), (0, False), (1, True), (1, False)]
PHASES = [("att", 0), ("att", 1), ("mlp", 0), ("att", 2), ("att", 3), ("mlp", 1)]
TU = {True: 1, False: 2}

FIELDS = [
    ("ln", 12),
    ("wq0", 512), ("bq0", 4), ("wk0", 512), ("bk0", 4), ("wv0", 128), ("bv0", 128), ("wo0", 512), ("bo0", 128),
    ("wq1", 512), ("bq1", 4), ("wk1", 512), ("bk1", 4), ("wv1", 128), ("bv1", 128), ("bv1_short", 128), ("wo1", 512), ("bo1", 128),
    ("w1_0", 512), ("b1_0", 4), ("w2_0", 512), ("b2_0", 128),
    ("wq2", INNER), ("wk2", INNER), ("wv2", INNER), ("wo2", INNER), ("bo2", 128),
    ("wq3", INNER), ("wk3", INNER), ("wv3", INNER), ("wo3", INNER), ("bo3", 128),
    ("w1_1", 2 * F), ("b1_1", 8), ("w2_1", 512), ("b2_1", 128),
]
AT, _at = {}, 0
for _name, _w in FIELDS:
    AT[_name] = (_at, _at + _w)
    _at += _w
WCOLS = _at
PARTS = [("ln", "wq1"), ("wq1", "w1_0"), ("w1_0", "wq2"), ("wq2", "wq3"), ("wq3", "w1_1"), ("w1_1", None)]


def steps(a):
    return 4 if ATT[a][0] == 0 else 8


def tiles_of(a):
    return TU[ATT[a][1]]


def units(a):
    return H * QT // tiles_of(a)


def per_step(a):
    return units(a) // steps(a)


def per_head(a):
    return QT // tiles_of(a)


LAG_E, LAG_N, LAG_T, LAG_C = 1, 2, 4, 5


def after_values(a):
    return LAG_C + per_head(a) * (1 if ATT[a][0] == 0 else 2)


RUNS = [(a, q) for a in range(4) for q in range(2)]
PHASE_OF = [0, 1, 3, 4]


def timetable():
    start, joins, norms, jobs, gelus = [], {}, {}, {}, {}

    def place(at, job, sparse=False):
        while at in jobs or (sparse and (at - start[4]) % per_step(2) != V_AT[2] + 2):
            at += 1
        jobs[at] = job
        return at

    def norm(n, q, at):
        norms[n, q] = at
        return place(at + 3, ("ln", n, q)) + 2

    def mlp(n, q, at):
        for m in range(4):
            at = place(at, ("gate", n, q, m), sparse=(n, q) == (2, 1)) + 1
        gelus[n, q] = at + 1
        at += 2
        if n == 5:
            for m in range(4):
                at = place(at, ("lin", n, q, m)) + 1
            at += 1
        while at in jobs or at + 1 in jobs:
            at += 1
        for half in range(2):
            jobs[at + half] = ("out", n, q, half)
        joins[n, q] = at + 2
        return joins[n, q]

    def follow(r):
        a, q = RUNS[r]
        n = PHASE_OF[a]
        joins[n, q] = start[r] + units(a) + after_values(a) + QT
        ready[q] = norm(n + 1, q, joins[n, q])
        if n + 1 in (2, 5):
            end = mlp(n + 1, q, ready[q])
            if n + 1 == 2:
                ready[q] = norm(3, q, end)

    ready = [norm(0, 0, 0), 0]
    for r, (a, q) in enumerate(RUNS):
        layer, own = ATT[a]
        before = RUNS[r - 1][0]
        at = start[-1] + units(before) if r else 0
        if r:
            at += max(0, after_values(before) - after_values(a))
        first = max(ready[q], at - (8 if layer == 0 else 4))
        if r == 4:
            first = max(first, start[3] + units(before) - 1)
        first = place(first, ("q", r, 0))
        first = place(first + 1, ("k", r, 0))
        if layer == 0:
            place(first + 1, ("v", r, 0))
        at = max(at, first + 2)
        start.append(at)
        for s in range(steps(a)):
            if layer == 0:
                place(at + per_step(a) * (s + 1) + after_values(a) - 3, ("scale", r, s))
            if layer == 1:
                place(at + per_step(a) * s + V_AT[a], ("v", r, s))
            if s < steps(a) - 1:
                place(at + per_step(a) * s + Q_AT[a], ("q", r, s + 1))
                place(at + per_step(a) * s + K_AT[a], ("k", r, s + 1))
        if r == 0:
            ready[1] = norm(0, 1, at + 6)
        else:
            follow(r - 1)
    follow(len(RUNS) - 1)
    last = max(list(joins.values()) + list(jobs)) + 2
    return start, joins, norms, sorted(jobs.items()), gelus, last


Q_AT, K_AT, V_AT = [0, 0, 0, 0], [4, 2, 2, 2], [None, None, 4, 1]
START, JOINS, NORMS, JOBS, GELUS, LAST = timetable()


def taker(job):
    if job[0] == "scale":
        return "scale"
    return "act" if job[0] == "v" and ATT[RUNS[job[1]][0]][0] == 1 else "dve"


BANK = {job: 0 for _, job in JOBS}
BANK["k", 0, 0] = 1
for _m in range(4):
    BANK["gate", 5, 1, _m] = BANK["lin", 5, 1, _m] = _m

INDEX, TAKEN, BEFORE, HI_INDEX = {}, {}, {}, {}
_last = {}
PER = {"dve": 0, "act": 0, "scale": 0}
PER_FILLED = 0
for _n, (_, _job) in enumerate(JOBS):
    part = _job[0] == "out" and _job[3] == 0
    PER[taker(_job)] += 0 if part else 1
    PER_FILLED += 0 if _job[0] == "scale" else 1
    INDEX[_job], TAKEN[_job] = PER_FILLED, PER[taker(_job)]
    BEFORE[_job] = None if _job[0] == "out" and _job[3] else _last.get(BANK[_job])
    _last[BANK[_job]] = _job
    if _job[0] in "qk":
        HI_INDEX[_job] = len(HI_INDEX) + 1
JOIN_INDEX = {key: n + 1 for n, key in enumerate(sorted(JOINS, key=JOINS.get))}
NORM_ORDER = sorted(NORMS, key=NORMS.get)
NORM_INDEX = {key: n + 1 for n, key in enumerate(NORM_ORDER)}
GELU_INDEX = {key: n + 1 for n, key in enumerate(sorted(GELUS, key=GELUS.get))}


def first_unit(r):
    return sum(units(a) for a, _ in RUNS[:r])


def unit_at(g):
    for r, (a, _) in enumerate(RUNS):
        if 0 <= g - START[r] < units(a):
            return r, g - START[r], first_unit(r) + g - START[r]
    return None


def jobs_at(g):
    return [job for at, job in JOBS if at == g]


def step_before(r, s, n):
    if s >= n:
        return r, s - n
    if r in (0, 4):
        return None
    return r - 1, steps(RUNS[r - 1][0]) + s - n


def sums_at(r, g):
    a = RUNS[r][0]
    i = g - START[r] - LAG_N - per_step(a) + 1
    s = i // per_step(a)
    return s if i % per_step(a) == 0 and 0 <= s < steps(a) else None


def values_at(r, g):
    a = RUNS[r][0]
    i = g - START[r]
    tiles = len(KT[ATT[a][1]])
    heads = 1 if ATT[a][0] == 0 else 2
    span = heads * per_head(a)
    n, rest = (i - LAG_C) // span - 1, (i - LAG_C) % span
    return [(heads * n * steps(a) // H, list(range(heads * n, heads * n + heads)), kt)
            for kt in range(tiles) if 0 <= heads * n < H and kt * span // tiles == rest]


def copy_at(r, g):
    a = RUNS[r][0]
    i = g - START[r] - after_values(a) + 1
    s = i // per_step(a) - 1
    return s if i % per_step(a) == 0 and 0 <= s < steps(a) else None


def result_at(r, g):
    a = RUNS[r][0]
    i = g - START[r] - after_values(a)
    s, t = i // per_step(a) - 1, i % per_step(a)
    return (s, t) if t < QT and 0 <= s < steps(a) else None


def events_at(table, g):
    return [key for key in table if table[key] == g]


def build(nc, x, ctx_t, wimg, out):
    with ExitStack() as ctx:
        def sb(name, shape, dt=F32):
            return ctx.enter_context(nc.sbuf_tensor(name, shape, dt))

        def psum(name, shape):
            return ctx.enter_context(nc.psum_tensor(name, shape, F32))

        def sem(name):
            return ctx.enter_context(nc.semaphore(name))

        w = sb("w", [128, WCOLS])
        ident = sb("ident", [128, 128])
        x_in = sb("x_in", [128, 2, QT, D])
        xs = sb("xs", [128, 2, QT, D])
        c_t = sb("c_t", [C, 2, 256])
        xn = sb("xn", [128, QT, D])
        stats = sb("stats", [128, QT, 6])
        mv = sb("mv", [128, QT, 2])
        var_eps = sb("var_eps", [128, QT])
        ones = sb("ones", [128, QT])
        minus_half = sb("minus_half", [128, QT])
        rstd = sb("rstd", [128, QT])
        wait_taker = sb("wait_taker", [128, 1])
        h_t = sb("h_t", [128, 2, S])
        q_parts = sb("q_parts", [128, 2, S], F32R)
        k_parts = sb("k_parts", [128, 2, S], F32R)
        k0 = sb("k0", [128, 2, 4, S], F32R)
        v0 = sb("v0", [128, 2, 4, 4, 160])
        q1 = sb("q1", [128, 2, 2, 2, S], F32R)
        k1 = sb("k1", [128, 2, 2, S], F32R)
        NV = 3
        v1 = sb("v1", [128, NV, 4, 128])
        NP, NPT, NR = 5, 4, 8
        p = sb("p", [128, NP, S])
        p_t = sb("p_t", [128, NPT, 4, S])
        neg_max = sb("neg_max", [128, NR, 2])
        sums = sb("sums", [128, 2, QT, 4])
        inverse = sb("inverse", [128, QT, 4])
        scales = sb("scales", [128, QT, 128])
        row_sum = sb("row_sum", [128, NR, 2])
        r_sum = sb("r_sum", [128, NR, 2])
        o_t = sb("o_t", [128, 2, S])
        hidden = sb("hidden", [128, 4, S])

        NS, NT = 3, 2
        ps_s = psum("ps_s", [128, NS, 512])
        ps_t = psum("ps_t", [128, NT, 512])
        ps_g = psum("ps_g", [128, 512])
        ps_o = psum("ps_o", [128, 512])
        ps_y = psum("ps_y", [128, 512])

        w_loaded = [sem(f"w_loaded{n}") for n in range(len(PARTS))]
        x_loaded = [sem("x_loaded0"), sem("x_loaded1")]
        c_loaded = [sem("c_loaded0"), sem("c_loaded1")]
        ident_done = sem("ident_done")
        zeros_done = sem("zeros_done")
        scale_done = sem("scale_done")
        c_zeroed = sem("c_zeroed")
        out_stored = [sem("out_stored0"), sem("out_stored1")]
        stats_done = sem("stats_done")
        mv_done = sem("mv_done")
        var_done = sem("var_done")
        rstd_done = sem("rstd_done")
        norm_done = sem("norm_done")
        bias_added = sem("bias_added")
        gen_filled = sem("gen_filled")
        scales_filled = sem("scales_filled")
        taken = {"dve": sem("taken_by_dve"), "act": sem("taken_by_act"), "scale": sem("scales_taken")}
        hi_done = sem("hi_done")
        k_spread = [sem("k_spread0"), sem("k_spread1")]
        q_moved = [sem("q_moved0"), sem("q_moved1")]
        k_moved = [sem("k_moved0"), sem("k_moved1")]
        gelu_done = sem("gelu_done")
        y_filled = sem("y_filled")
        residual_done = sem("residual_done")
        scores_ready = sem("scores_ready")
        max_ready = sem("max_ready")
        exp_ready = sem("exp_ready")
        recip_done = sem("recip_done")
        inverse_ready = sem("inverse_ready")
        scales_ready = sem("scales_ready")
        probs_ready = sem("probs_ready")
        pt_filled = sem("pt_filled")
        pt_copied = sem("pt_copied")
        o_filled = sem("o_filled")
        o_copied = sem("o_copied")

        def bank_of(job):
            return ps_s[:, BANK[job] - 1, :] if BANK[job] else ps_g[:]

        def W(name, lo=0, hi=None, rows=128):
            a, z = AT[name]
            return w[0:rows, a + lo:(z if hi is None else a + hi)]

        PER_O = sum(steps(a) for a, _ in RUNS)
        PER_UNIT = first_unit(len(RUNS))
        UNITS_1 = first_unit(4)
        PER_SCALE = 4 * 4
        PER_NORM = len(NORMS)
        PER_SPREAD = 4 * 2 * 64
        PER_Q_MOVED = 4 * 4 * 64
        PER_K_MOVED = 2 * 4 * 64

        def wait_taken(eng, b, job):
            who = taker(job)
            eng.wait_ge(taken[who], b * PER[who] + TAKEN[job])

        def wait_filled(eng, b, job):
            if job[0] == "scale":
                eng.wait_ge(scales_filled, b * PER_SCALE + TAKEN[job])
            else:
                eng.wait_ge(gen_filled, b * PER_FILLED + INDEX[job])

        def wait_hi(eng, b, job):
            eng.wait_ge(hi_done, b * len(HI_INDEX) + HI_INDEX[job])

        def wait_q_moved(eng, b, r, s):
            eng.wait_ge(q_moved[s % 2], b * PER_Q_MOVED + 64 * (4 * (r - 4) + s // 2 + 1))

        def wait_k_moved(eng, b, r, s):
            eng.wait_ge(k_moved[s % 2], b * PER_K_MOVED + 64 * (4 * (r - 4) + s // 2 + 1))

        def wait_spread(eng, b, r, s):
            eng.wait_ge(k_spread[s % 2], b * PER_SPREAD + 64 * (2 * r + s // 2 + 1))

        def unit_wait(eng, semaphore, b, n):
            eng.wait_ge(semaphore, b * PER_UNIT + n + 1)

        def unit_wait_1(eng, semaphore, b, n):
            eng.wait_ge(semaphore, b * (PER_UNIT - UNITS_1) + n - UNITS_1 + 1)

        def step_wait(eng, b, r, s):
            unit_wait(eng, scores_ready, b, first_unit(r) + per_step(RUNS[r][0]) * (s + 1) - 1)

        def step_index(r, s):
            return sum(steps(a) for a, _ in RUNS[:r]) + s + 1

        def wait_weights(eng, g):
            for part in range(2, len(PARTS)):
                if g == 16 * part:
                    eng.wait_ge(w_loaded[part], 16)

        block = ctx.enter_context(nc.Block())

        @block.sync
        def _(sp):
            for n, (first, end) in enumerate(PARTS):
                lo, hi = AT[first][0], (AT[end][0] if end else WCOLS)
                sp.dma_start(w[:, lo:hi], wimg[:, lo:hi]).then_inc(w_loaded[n], 16)
            with sp.Fori(0, B // 2) as b:
                for _, job in JOBS:
                    kind, r, s = job[:3]
                    if kind not in "qk":
                        continue
                    layer, own = ATT[RUNS[r][0]]
                    nk = S if own else SK
                    if layer == 0 and kind == "k":
                        wait_taken(sp, b, job)
                        for j in range(4):
                            sp.dma_start(k0[j:128:4, s % 2, j, 0:nk].bitcast(F32),
                                         k_parts[j:128:4, s % 2, 0:nk].bitcast(F32)).then_inc(k_spread[s % 2], 16)
                    if layer == 1 and kind == "q":
                        wait_taken(sp, b, job)
                        for e in range(2):
                            for row in (0, 64):
                                sp.dma_start(q1[row:row + 64, s % 2, e].bitcast(F32),
                                             q_parts[64 * e:64 * e + 64].bitcast(F32)).then_inc(q_moved[s % 2], 16)
                    if layer == 1 and own and kind == "k":
                        wait_taken(sp, b, job)
                        for e in range(2):
                            for part in range(2):
                                sp.dma_start(k1[64 * part:64 * part + 64, s % 2, e, 0:nk].bitcast(F32),
                                             k_parts[64 * e:64 * e + 64, part, 0:nk].bitcast(F32)).then_inc(
                                                 k_moved[s % 2], 16)

        @block.gpsimd
        def _(pool):
            pool.memset(c_t[:], 0.0).then_inc(c_zeroed, 1)
            pool.dma_start(x_in[:, 0], x[0, 0].rearrange("(t p) d -> p t d", p=128)).then_inc(x_loaded[0], 16)
            pool.dma_start(x_in[:, 1], x[0, 1].rearrange("(t p) d -> p t d", p=128)).then_inc(x_loaded[1], 16)
            pool.wait_ge(c_zeroed, 1)
            for q in range(2):
                pool.dma_start(c_t[:, q, 0:SK], ctx_t[0, q]).then_inc(c_loaded[q], 16)
            pool.memset(ones[:], 1.0).then_inc(ident_done, 1)
            pool.memset(minus_half[:], -0.5).then_inc(ident_done, 1)
            pool.memset(ident[:], 0.0).then_inc(ident_done, 1)
            pool.wait_ge(ident_done, 3)
            pool.affine_select(out=ident[:], in_=ident[:], compare_op=ALU.not_equal, fill=1.0, base=0,
                               pattern=[[-1, 128]], channel_multiplier=1).then_inc(ident_done, 1)
            for part in (0, 1):
                pool.wait_ge(w_loaded[part], 16)
            with pool.Fori(0, B // 2) as b:
                for g in range(LAST):
                    wait_weights(pool, g)
                    for n, q in events_at(NORMS, g - 1):
                        pool.wait_ge(var_done, b * PER_NORM + NORM_INDEX[n, q])
                        pool.tensor_tensor(rstd[:], var_eps[:], minus_half[:], ALU.pow).then_inc(rstd_done, 1)
                    for n, q in events_at(NORMS, g - 2):
                        kind, a = PHASES[n]
                        pool.wait_ge(norm_done, b * PER_NORM + NORM_INDEX[n, q])
                        bias = W(f"bo{a}") if kind == "att" else W(f"b2_{a}")
                        pool.tensor_tensor(xs[:, q], x_in[:, q] if n == 0 else xs[:, q],
                                           bias[:, None, :].to_broadcast([128, QT, D]), ALU.add).then_inc(bias_added, 1)
                        if n == 0:
                            pool.wait_ge(bias_added, b * PER_NORM + NORM_INDEX[n, q])
                            pool.dma_start(x_in[:, q], x[1:B // 2 + 1][b][q].rearrange(
                                "(t p) d -> p t d", p=128)).then_inc(x_loaded[q], 16)
                    for r in range(4):
                        s = sums_at(r, g)
                        if s is not None:
                            pool.wait_ge(inverse_ready, b * PER_SCALE + 4 * r + s + 1)
                            if r + s > 0:
                                pool.wait_ge(o_copied, b * PER_O + step_index(r, s) - 1)
                            repeated = inverse[:, :, :, None].to_broadcast([128, QT, 4, 8])
                            for kt in range(4):
                                last = pool.tensor_tensor(
                                    scales[:, :, 32 * kt:32 * kt + 32].rearrange("q t (j d) -> q t j d", j=4),
                                    repeated, ones[:, :, None, None].to_broadcast([128, QT, 4, 8]), ALU.mult)
                            last.then_inc(scales_ready, 1)
                for q in range(2):
                    wait_taken(pool, b, ("v", 6 + q, 7))
                    pool.dma_start(c_t[:, q, 0:SK], ctx_t[1:B // 2 + 1][b][q]).then_inc(c_loaded[q], 16)
                for q in range(2):
                    pool.wait_ge(residual_done, b * len(JOINS) + JOIN_INDEX[5, q])
                    pool.dma_start(out[b][q].rearrange("(t p) d -> p t d", p=128), xs[:, q]).then_inc(out_stored[q], 16)
                for q in range(2):
                    pool.wait_ge(out_stored[q], b * 16 + 16)
            for q in range(2):
                pool.wait_ge(out_stored[q], 16 * (B // 2))
                pool.wait_ge(x_loaded[q], 16 * (B // 2 + 1))
                pool.wait_ge(c_loaded[q], 16 * (B // 2 + 1))

        @block.tensor
        def _(pe):
            def norm_transposes(b, n, q):
                pe.wait_ge(norm_done, b * PER_NORM + NORM_INDEX[n, q])
                for t in range(QT):
                    last = pe.transpose(ps_g[:, 128 * t:128 * t + 128], xn[:, t, :], ident[:])
                return last

            def source(r, kind):
                a, q = RUNS[r]
                if kind == "q" or ATT[a][1]:
                    return 128, h_t[:, q, :], S
                return C, c_t[:, q, :], SK

            def wait_source(b, r, kind):
                a, q = RUNS[r]
                if kind == "q" or ATT[a][1]:
                    wait_taken(pe, b, ("ln", PHASE_OF[a], q))
                else:
                    pe.wait_ge(c_loaded[q], b * 16 + 16)

            def qk_product(kind, r, s):
                a = RUNS[r][0]
                bank = bank_of((kind, r, s))
                rows, src, nk = source(r, kind)
                if a == 3 and kind == "k":
                    for e in range(2):
                        for row in (0, 64):
                            last = pe.matmul(bank[row:row + 64, nk * e:nk * e + nk],
                                             W("wk3", 64 * (2 * s + e), 64 * (2 * s + e) + 64, rows), src[:, 0:nk],
                                             start=True, stop=True)
                    return last
                return pe.matmul(bank[:, 0:nk], W(f"w{kind}{a}", 128 * s, 128 * s + 128, rows), src[:, 0:nk],
                                 start=True, stop=True)

            def v_product(r, s):
                a = RUNS[r][0]
                layer, own = ATT[a]
                rows, src, _ = source(r, "v")
                for kt in range(len(KT[own])):
                    last = pe.matmul(ps_g[:, 128 * kt:128 * kt + 128], src[:, 128 * kt:128 * kt + 128],
                                     W(f"wv{a}", 128 * s, 128 * s + 128, rows), start=True, stop=True)
                return last

            def result(bank, acts, weights, rows, t, first, last):
                return pe.matmul(bank[:, 128 * t:128 * t + 128], acts[0:rows, 128 * t:128 * t + 128], weights,
                                 start=first and t == 0, stop=last, skip_group_check=True)

            def mlp_result(b, n, q, half):
                a = PHASES[n][1]
                if half == 0:
                    if a == 0:
                        pe.wait_ge(gelu_done, b * len(GELUS) + GELU_INDEX[n, q])
                    else:
                        wait_taken(pe, b, ("lin", n, q, 3))
                for t in (2 * half, 2 * half + 1):
                    for m in range(4):
                        last = result(ps_g, hidden[:, m], W(f"w2_{a}", 128 * m, 128 * m + 128), 128, t, m == 0, m == 3)
                return last

            def product(b, job):
                kind = job[0]
                if BEFORE[job]:
                    wait_taken(pe, b, BEFORE[job])
                if kind == "gate" and BANK[job]:
                    unit_wait(pe, exp_ready, b, PER_UNIT - 1)
                if kind == "ln":
                    last = norm_transposes(b, *job[1:])
                elif kind in "qk":
                    wait_source(b, job[1], kind)
                    last = qk_product(*job)
                elif kind == "v":
                    wait_source(b, job[1], kind)
                    last = v_product(*job[1:])
                elif kind == "scale":
                    r, s = job[1:]
                    pe.wait_ge(scales_ready, b * PER_SCALE + 4 * r + s + 1)
                    for t in range(QT):
                        last = pe.transpose(ps_g[:, 128 * t:128 * t + 128], scales[:, t, :], ident[:])
                elif kind == "out":
                    last = mlp_result(b, *job[1:])
                else:
                    n, q, m = job[1:]
                    a = PHASES[n][1]
                    wait_taken(pe, b, ("ln", n, q))
                    off = 128 * m + (F if a == 1 and kind == "gate" else 0)
                    last = pe.matmul(bank_of(job), W(f"w1_{a}", off, off + 128), h_t[:, q, :], start=True, stop=True)
                last.then_inc(scales_filled if kind == "scale" else gen_filled, 1)

            def scores(b, r, i, n):
                a = RUNS[r][0]
                layer, own = ATT[a]
                nk, tu = S if own else SK, TU[own]
                h, part = divmod(i, per_head(a))
                s = i // per_step(a)
                if i % per_step(a) == 0:
                    if layer == 0:
                        wait_taken(pe, b, ("q", r, s))
                        wait_spread(pe, b, r, s)
                    else:
                        wait_q_moved(pe, b, r, s)
                        if own:
                            wait_k_moved(pe, b, r, s)
                        else:
                            wait_taken(pe, b, ("k", r, s))
                if n >= NS:
                    unit_wait(pe, exp_ready, b, n - NS)
                for t in range(tu):
                    bank = ps_s[:, n % NS, nk * t:nk * t + nk]
                    cols = slice(128 * (part * tu + t), 128 * (part * tu + t) + 128)
                    if layer == 0:
                        last = pe.matmul(bank, q_parts[:, s % 2, cols], k0[:, s % 2, h % 4, 0:nk],
                                         start=True, stop=True)
                    else:
                        for half in range(2):
                            last = pe.matmul(bank, q1[:, s % 2, h % 2, half, cols], k1[:, s % 2, h % 2, 0:nk],
                                             start=half == 0, stop=half == 1)
                last.then_inc(scores_ready, 1)

            def values(b, r, s, heads, kt):
                a, q = RUNS[r]
                layer, own = ATT[a]
                tiles = len(KT[own])
                first = kt == 0 and (layer == 1 or heads[0] % 4 == 0)
                full = kt == tiles - 1 and (layer == 1 or heads[0] % 4 == 3)
                if kt == 0:
                    unit_wait(pe, pt_copied, b, first_unit(r) + per_head(a) * (heads[-1] + 1) - 1)
                    if layer == 1 or heads[0] == 0:
                        wait_taken(pe, b, ("v", r, s if layer == 1 else 0))
                if first and step_index(r, s) > 1:
                    pe.wait_ge(o_copied, b * PER_O + step_index(r, s) - 1)
                for h in heads:
                    if layer == 0:
                        last = pe.matmul(ps_o[32 * kt:32 * kt + 32, :], v0[:, q, kt, h // 4, 32 * (h % 4):32 * (h % 4) + 32],
                                         p_t[:, h % NPT, kt, :],
                                         start=h % 4 == 0, stop=h % 4 == 3, skip_group_check=True)
                    else:
                        row = 64 * (h % 2)
                        last = pe.matmul(ps_o[row:row + 64, :], v1[:, step_index(r, s) % NV, kt, row:row + 64],
                                         p_t[:, h % NPT, kt, :], start=kt == 0, stop=kt == tiles - 1)
                if full:
                    last.then_inc(o_filled, 1)

            def prob_transposes(b, r, n):
                own = ATT[RUNS[r][0]][1]
                nk, tu = S if own else SK, TU[own]
                if r < 4:
                    unit_wait(pe, exp_ready, b, n)
                else:
                    unit_wait_1(pe, probs_ready, b, n)
                if n >= NT:
                    unit_wait(pe, pt_copied, b, n - NT)
                for kt, (k0_, kn) in enumerate(KT[own]):
                    for t in range(tu):
                        at = 128 * (kt * tu + t)
                        last = pe.transpose(ps_t[0:kn, n % NT, at:at + 128],
                                            p[:, n % NP, nk * t + k0_:nk * t + k0_ + kn], ident[:])
                last.then_inc(pt_filled, 1)

            def output(b, r, s, t):
                a = RUNS[r][0]
                layer, own = ATT[a]
                rows = 128 if layer == 1 else 32 * len(KT[own])
                if t == 0:
                    pe.wait_ge(o_copied, b * PER_O + step_index(r, s))
                    if s == 0 and r > 0:
                        before, q = RUNS[r - 1]
                        pe.wait_ge(residual_done, b * len(JOINS) + JOIN_INDEX[PHASE_OF[before], q])
                end = s == steps(a) - 1
                last = result(ps_y, o_t[:, s % 2], W(f"wo{a}", 128 * s, 128 * s + 128, rows), rows, t, s == 0, end)
                if end and t == QT - 1:
                    last.then_inc(y_filled, 1)

            pe.wait_ge(ident_done, 4)
            for part in (0, 1):
                pe.wait_ge(w_loaded[part], 16)
            pe.wait_ge(scale_done, 4)
            pe.wait_ge(zeros_done, 2)
            with pe.Fori(0, B // 2) as b:
                for g in range(LAST):
                    wait_weights(pe, g)
                    if unit_at(g):
                        scores(b, *unit_at(g))
                    for r in range(len(RUNS)):
                        for s, heads, kt in values_at(r, g):
                            values(b, r, s, heads, kt)
                    if unit_at(g - LAG_T):
                        r, _, n = unit_at(g - LAG_T)
                        prob_transposes(b, r, n)
                    for r in range(len(RUNS)):
                        if result_at(r, g):
                            output(b, r, *result_at(r, g))
                    for job in jobs_at(g):
                        product(b, job)

        @block.scalar
        def _(act):
            def hi_part(b, job):
                kind, r, s = job
                a = RUNS[r][0]
                layer, own = ATT[a]
                nk = S if kind == "q" or own else SK
                wait_filled(act, b, job)
                bank = bank_of(job)
                parts = q_parts if kind == "q" else k_parts
                if layer == 0:
                    if step_before(r, s, 2) and kind == "q":
                        step_wait(act, b, *step_before(r, s, 2))
                    if step_before(r, s, 2) and kind == "k":
                        wait_spread(act, b, *step_before(r, s, 2))
                    act.activation(parts[:, s % 2, 0:nk], bank[:, 0:nk], ACT.Identity, bias=W(f"b{kind}{a}", s, s + 1),
                                   scale=1.0).then_inc(hi_done, 1)
                elif a == 3 and kind == "k":
                    step_wait(act, b, *step_before(r, s, 2))
                    act.activation(k1[:, s % 2, :, 0:nk], bank[:, 0:2 * nk].rearrange("d (e k) -> d e k", e=2),
                                   ACT.Copy).then_inc(hi_done, 1)
                else:
                    if step_before(r, s, 1):
                        (wait_q_moved if kind == "q" else wait_k_moved)(act, b, *step_before(r, s, 1))
                    act.activation(parts[:, 0, 0:nk], bank[:, 0:nk], ACT.Copy,
                                   scale=HD[1] ** -0.5 if kind == "q" else 1.0).then_inc(hi_done, 1)

            def copy_transposed(b, r, i, n):
                a = RUNS[r][0]
                own = ATT[a][1]
                tu = TU[own]
                h, part = divmod(i, per_head(a))
                cols = slice(128 * tu * part, 128 * tu * (part + 1))
                unit_wait(act, pt_filled, b, n)
                if own:
                    act.activation(p_t[:, h % NPT, :, cols], ps_t[:, n % NT, :].rearrange("k (n q) -> k n q", n=4),
                                   ACT.Copy).then_inc(pt_copied, 1)
                else:
                    kn = SK - 128
                    act.activation(p_t[:, h % NPT, 0, cols], ps_t[:, n % NT, 0:256], ACT.Copy)
                    act.activation(p_t[0:kn, h % NPT, 1, cols], ps_t[0:kn, n % NT, 256:512],
                                   ACT.Copy).then_inc(pt_copied, 1)

            def exps(b, r, i, n):
                a = RUNS[r][0]
                own = ATT[a][1]
                h, part = divmod(i, per_head(a))
                nk, tu = S if own else SK, TU[own]
                unit_wait(act, max_ready, b, n)
                if n >= NP:
                    unit_wait(act, pt_filled, b, n - NP)
                for t in range(tu):
                    total = (sums[:, h // 4 % 2, part * tu + t, h % 4:h % 4 + 1] if r < 4 else
                             row_sum[:, n % NR, t:t + 1])
                    last = act.activation(p[:, n % NP, nk * t:nk * t + nk], ps_s[:, n % NS, nk * t:nk * t + nk],
                                          ACT.Exp, bias=neg_max[:, n % NR, t:t + 1], scale=1.0,
                                          accum_out=total)
                last.then_inc(exp_ready, 1)

            for part in (0, 1):
                act.wait_ge(w_loaded[part], 16)
            act.wait_ge(zeros_done, 2)
            with act.Fori(0, B // 2) as b:
                for g in range(LAST):
                    if unit_at(g - LAG_E):
                        exps(b, *unit_at(g - LAG_E))
                    for job in jobs_at(g - 1):
                        if job[0] in "qk":
                            hi_part(b, job)
                        if job[0] == "v" and taker(job) == "act":
                            r, s = job[1:]
                            tiles = len(KT[ATT[RUNS[r][0]][1]])
                            wait_filled(act, b, job)
                            act.activation(v1[:, step_index(r, s) % NV, 0:tiles, :],
                                           ps_g[:, 0:128 * tiles].rearrange("k (t n) -> k t n", t=tiles),
                                           ACT.Copy).then_inc(taken["act"], 1)
                        if job[0] == "scale":
                            wait_filled(act, b, job)
                            act.activation(scales[:].rearrange("r t q -> r (t q)"), ps_g[:], ACT.Copy).then_inc(taken["scale"], 1)
                    if unit_at(g - LAG_C):
                        copy_transposed(b, *unit_at(g - LAG_C))
                    for n, q in events_at(GELUS, g):
                        wait_taken(act, b, ("gate", n, q, 3))
                        act.activation(hidden[:], hidden[:], ACT.Gelu).then_inc(gelu_done, 1)

        @block.vector
        def _(dve):
            def take(b, job):
                kind = job[0]
                wait_filled(dve, b, job)
                bank = bank_of(job)
                if kind == "ln":
                    n, q = job[1:]
                    return dve.tensor_scalar(h_t[:, q, :], bank, W("ln", 2 * n, 2 * n + 1),
                                             W("ln", 2 * n + 1, 2 * n + 2), ALU.mult, ALU.add).then_inc(taken["dve"], 1)
                if kind == "gate":
                    n, q, m = job[1:]
                    a = PHASES[n][1]
                    return dve.tensor_scalar(hidden[:, m, :], bank, W(f"b1_{a}", 4 * a + m, 4 * a + m + 1), None,
                                             ALU.add).then_inc(taken["dve"], 1)
                if kind == "lin":
                    n, q, m = job[1:]
                    dve.wait_ge(gelu_done, b * len(GELUS) + GELU_INDEX[n, q])
                    return dve.scalar_tensor_tensor(out=hidden[:, m, :], in0=bank, scalar=W("b1_1", m, m + 1),
                                                    in1=hidden[:, m, :], op0=ALU.add,
                                                    op1=ALU.mult).then_inc(taken["dve"], 1)
                r, s = job[1:]
                a, q = RUNS[r]
                layer, own = ATT[a]
                if kind == "v":
                    for kt in range(len(KT[own])):
                        bias = W("bv1_short" if a == 1 and kt == 1 else f"bv{a}")
                        last = dve.tensor_tensor(
                            v0[:, q, kt].rearrange("k g (j n) -> k g j n", j=4)[:, :, :, 0:8],
                            bank[:, 128 * kt:128 * kt + 128].rearrange("k (g j d) -> k g j d", j=4, d=8),
                            bias.rearrange("k (g j d) -> k g j d", j=4, d=8), ALU.add)
                    return last.then_inc(taken["dve"], 1)
                wait_hi(dve, b, job)
                nk = S if kind == "q" or own else SK
                src = bank[:, 0:nk]
                parts = q_parts if kind == "q" else k_parts
                if layer == 0:
                    bias = W(f"b{kind}{a}", s, s + 1)
                    dst = parts[:, s % 2, 0:nk]
                    for row, n in ([(64, 64)] if kind == "q" else [(32, 32), (96, 32)]):
                        last = dve.scalar_tensor_tensor(out=dst[row:row + n], in0=src[row:row + n],
                                                        scalar=bias[row:row + n], in1=dst[row:row + n].bitcast(F32),
                                                        op0=ALU.add, op1=ALU.subtract)
                    return last.then_inc(taken["dve"], 1)
                if a == 3 and kind == "k":
                    dst = k1[64:128, s % 2, :, 0:nk]
                    return dve.tensor_tensor(dst, bank[64:128, 0:2 * nk].rearrange("d (e k) -> d e k", e=2),
                                             dst.bitcast(F32), ALU.subtract).then_inc(taken["dve"], 1)
                return dve.scalar_tensor_tensor(out=parts[:, 1, 0:nk], in0=src,
                                                scalar=HD[1] ** -0.5 if kind == "q" else 1.0,
                                                in1=parts[:, 0, 0:nk].bitcast(F32), op0=ALU.mult,
                                                op1=ALU.subtract).then_inc(taken["dve"], 1)

            def join(b, n, q):
                kind, a = PHASES[n]
                dve.wait_ge(bias_added, b * PER_NORM + NORM_INDEX[n, q])
                if kind == "att":
                    dve.wait_ge(y_filled, b * len(RUNS) + RUNS.index((a, q)) + 1)
                    bank = ps_y
                else:
                    wait_filled(dve, b, ("out", n, q, 1))
                    bank = ps_g
                last = dve.tensor_tensor(xs[:, q], bank[:].rearrange("q (t n) -> q t n", t=QT), xs[:, q],
                                         ALU.add).then_inc(residual_done, 1)
                if kind == "mlp":
                    dve.wait_ge(residual_done, b * len(JOINS) + JOIN_INDEX[n, q])
                    dve.memset(wait_taker[:], 0.0).then_inc(taken["dve"], 1)

            def norm_stats(b, n, q):
                if n == 0:
                    dve.wait_ge(x_loaded[q], b * 16 + 16)
                else:
                    dve.wait_ge(residual_done, b * len(JOINS) + JOIN_INDEX[n - 1, q])
                src = x_in if n == 0 else xs
                for t in range(QT):
                    last = dve.bn_stats(stats[:, t, :], src[:, q, t, :])
                last.then_inc(stats_done, 1)

            def norm_variance(b, n, q):
                dve.wait_ge(stats_done, b * PER_NORM + NORM_INDEX[n, q])
                dve.memset(wait_taker[:], 0.0)
                for t in range(QT):
                    last = dve.bn_aggr(mv[:, t, :], stats[:, t, :])
                last.then_inc(mv_done, 1)
                dve.wait_ge(mv_done, b * PER_NORM + NORM_INDEX[n, q])
                dve.tensor_scalar(var_eps[:], mv[:, :, 1], EPS, None, ALU.add).then_inc(var_done, 1)

            def norm_apply(b, n, q):
                src = x_in if n == 0 else xs
                dve.wait_ge(rstd_done, b * PER_NORM + NORM_INDEX[n, q])
                for t in range(QT):
                    last = dve.tensor_scalar(xn[:, t, :], src[:, q, t, :], mv[:, t, 0:1], rstd[:, t:t + 1],
                                             ALU.subtract, ALU.mult)
                last.then_inc(norm_done, 1)

            def maxima(b, r, n):
                own = ATT[RUNS[r][0]][1]
                nk, tu = S if own else SK, TU[own]
                unit_wait(dve, scores_ready, b, n)
                dve.tensor_reduce(neg_max[:, n % NR, 0:tu],
                                  ps_s[:, n % NS, 0:tu * nk].rearrange("q (t k) -> q t k", t=tu),
                                  AX.X, ALU.max, negate=True).then_inc(max_ready, 1)

            def normalise(b, r, n):
                own = ATT[RUNS[r][0]][1]
                nk, tu = S if own else SK, TU[own]
                unit_wait(dve, exp_ready, b, n)
                dve.reciprocal(r_sum[:, n % NR, 0:tu], row_sum[:, n % NR, 0:tu]).then_inc(recip_done, 1)
                unit_wait_1(dve, recip_done, b, n)
                for t in range(tu):
                    part = p[:, n % NP, nk * t:nk * t + nk]
                    last = dve.tensor_scalar(part, part, r_sum[:, n % NR, t:t + 1], None, ALU.mult)
                last.then_inc(probs_ready, 1)

            dve.memset(k0[:].bitcast(F32), 0.0).then_inc(zeros_done, 1)
            dve.memset(v0[:], 0.0).then_inc(zeros_done, 1)
            for part in (0, 1):
                dve.wait_ge(w_loaded[part], 16)
            for a in range(2):
                dve.tensor_scalar(W(f"wq{a}"), W(f"wq{a}"), HD[0] ** -0.5, None, ALU.mult).then_inc(scale_done, 1)
                dve.tensor_scalar(W(f"bq{a}"), W(f"bq{a}"), HD[0] ** -0.5, None, ALU.mult).then_inc(scale_done, 1)
            dve.wait_ge(scale_done, 4)
            dve.wait_ge(zeros_done, 2)
            with dve.Fori(0, B // 2) as b:
                for g in range(LAST):
                    wait_weights(dve, g)
                    if unit_at(g - LAG_N) and unit_at(g - LAG_N)[0] >= 4:
                        r, _, n = unit_at(g - LAG_N)
                        normalise(b, r, n)
                    if unit_at(g):
                        r, _, n = unit_at(g)
                        maxima(b, r, n)
                    for r in range(4):
                        s = sums_at(r, g)
                        if s is not None:
                            unit_wait(dve, exp_ready, b, first_unit(r) + per_step(RUNS[r][0]) * (s + 1) - 1)
                            if r + s > 0:
                                dve.wait_ge(scales_ready, b * PER_SCALE + 4 * r + s)
                            dve.reciprocal(inverse[:], sums[:, s % 2]).then_inc(inverse_ready, 1)
                    for n, q in events_at(JOINS, g):
                        join(b, n, q)
                    for job in jobs_at(g - 1):
                        if taker(job) == "dve" and job[0] != "out":
                            take(b, job)
                    for n, q in events_at(NORMS, g - 2):
                        norm_apply(b, n, q)
                    for n, q in events_at(NORMS, g - 1):
                        norm_variance(b, n, q)
                    for n, q in events_at(NORMS, g):
                        norm_stats(b, n, q)
                    for r in range(len(RUNS)):
                        s = copy_at(r, g)
                        if s is not None:
                            layer, own = ATT[RUNS[r][0]]
                            rows = 128 if layer == 1 else 32 * len(KT[own])
                            dve.wait_ge(o_filled, b * PER_O + step_index(r, s))
                            if layer == 0:
                                wait_taken(dve, b, ("scale", r, s))
                                dve.tensor_tensor(o_t[0:rows, s % 2, :], ps_o[0:rows, :],
                                                  scales[0:rows].rearrange("r t q -> r (t q)"), ALU.mult).then_inc(o_copied, 1)
                            else:
                                dve.tensor_copy(o_t[0:rows, s % 2, :], ps_o[0:rows, :]).then_inc(o_copied, 1)


def kernel(**inputs):
    import numpy as np
    import concourse.bacc as bacc
    from concourse.bass_utils import run_bass_kernel_spmd

    f = {name: np.asarray(a) for name, a in inputs.items()}

    def full(a):
        return np.concatenate([a, np.zeros((128 - a.shape[0], a.shape[1]), a.dtype)]) if a.shape[0] < 128 else a

    def by_head(wt):
        v = wt.reshape(wt.shape[0], 4, 1, 4, 8).transpose(0, 1, 2, 4, 3)
        return np.broadcast_to(v, (wt.shape[0], 4, 4, 8, 4)).reshape(wt.shape[0], 512)

    def rows(v):
        return np.broadcast_to(v[None, :], (128, v.shape[0]))

    def cols(v):
        return v.reshape(-1, 128).T

    img = {}
    lns = ["L0_xattn_ln1", "L0_xattn_ln2", "L0_xattn_ln3"]
    pairs = [(f[n + "_g"], f[n + "_b"]) for n in lns] + [(f[f"L1_xattn_g{n}"], f[f"L1_xattn_b{n}"]) for n in (1, 2, 3)]
    img["ln"] = np.stack([v for pair in pairs for v in pair], axis=1)
    for a, pre in enumerate(("L0_xattn_sa_", "L0_xattn_ca_")):
        for k in "qk":
            img[f"w{k}{a}"] = full(by_head(f[pre + "w" + k].T))
            img[f"b{k}{a}"] = by_head(f[pre + "b" + k][None, :]).reshape(4, 128).T
        img[f"wv{a}"] = full(f[pre + "wv"].T)
        img[f"bv{a}"] = rows(f[pre + "bv"])
        if a == 1:
            img["bv1_short"] = full(rows(f[pre + "bv"])[:SK - 128])
        wo = np.broadcast_to(f[pre + "wo"].T.reshape(4, 1, 32, 128), (4, 4, 32, 128)).reshape(4, 128, 128)
        img[f"wo{a}"] = wo.transpose(1, 0, 2).reshape(128, 512)
        img[f"bo{a}"] = rows(f[pre + "bo"])
    img["w1_0"] = f["L0_xattn_mlp_w1"].T
    img["b1_0"] = cols(f["L0_xattn_mlp_b1"])
    img["w2_0"] = f["L0_xattn_mlp_w2"].T.reshape(4, 128, 128).transpose(1, 0, 2).reshape(128, 512)
    img["b2_0"] = rows(f["L0_xattn_mlp_b2"])
    for a, n in ((2, 1), (3, 2)):
        for k in "qkv":
            img[f"w{k}{a}"] = full(f[f"L1_xattn_W{k}{n}"])
        img[f"wo{a}"] = f[f"L1_xattn_Wo{n}"].reshape(8, 128, 128).transpose(1, 0, 2).reshape(128, 1024)
        img[f"bo{a}"] = rows(f[f"L1_xattn_bo{n}"])
    img["w1_1"] = f["L1_xattn_Wp"]
    img["b1_1"] = cols(f["L1_xattn_bp"])
    img["w2_1"] = f["L1_xattn_Wf"].reshape(4, 128, 128).transpose(1, 0, 2).reshape(128, 512)
    img["b2_1"] = rows(f["L1_xattn_bf"])
    wimg = np.ascontiguousarray(np.concatenate([img[name] for name, _ in FIELDS], axis=1))
    arrays = {
        "x_dram": np.ascontiguousarray(np.concatenate([f["x"], f["x"][:2]])).reshape(B // 2 + 1, 2, S, D),
        "ctx_t_dram": np.ascontiguousarray(np.concatenate([f["ctx_768"], f["ctx_768"][:2]]).transpose(
            0, 2, 1)).reshape(B // 2 + 1, 2, C, SK),
        "wimg_dram": wimg,
    }
    nc = bacc.Bacc("TRN2", target_bir_lowering=False, num_devices=1)
    args = [nc.dram_tensor(name, a.shape, mybir.dt.from_np(a.dtype), kind="ExternalInput").ap()
            for name, a in arrays.items()]
    out = nc.dram_tensor("out_dram", (B // 2, 2, S, D), F32, kind="ExternalOutput").ap()
    build(nc, *args, out)
    r = run_bass_kernel_spmd(nc, [arrays], core_ids=[0])
    return r.results[0]["out_dram"].reshape(B, S, D)
```
